# Optimizing a Trainium2 kernel written in Bass

```python
import numpy as np
import jax
import jax.numpy as jnp

def _softmax(x, axis=-1):
    return jax.nn.softmax(x, axis=axis)

def _gelu(x):
    return jax.nn.gelu(x, approximate=True)

def _silu(x):
    return jax.nn.silu(x)

def _sigmoid(x):
    return jax.nn.sigmoid(x)

def _layernorm(x, axis=-1, eps=1e-05):
    m = jnp.mean(x, axis=axis, keepdims=True)
    v = jnp.var(x, axis=axis, keepdims=True)
    return (x - m) / jnp.sqrt(v + eps)

def _scatter_add(tgt, idx, src, axis=0):
    return tgt.at[idx].add(src)

def _segment_sum(src, seg, n):
    return jax.ops.segment_sum(src, seg, n)
kernel_name = 'mk_adaln_d1_jaxref_r8_7cd114'

def setup_inputs(seed: int=0):
    np.random.seed(seed)
    _w = jnp.asarray

    def _L0_attn_setup():
        import jax, jax.numpy as jnp
        import numpy as np
        import math
        D_MODEL = 256
        NUM_HEADS = 16
        HEAD_DIM = D_MODEL // NUM_HEADS
        key = jax.random.key(seed)
        k_x, k_wqkv, k_bqkv, k_wo, k_bo = jax.random.split(key, 5)
        B, S = (2, 256)
        scale = 1.0 / math.sqrt(D_MODEL)
        return {'x': jax.random.normal(k_x, (B, S, D_MODEL), dtype=jnp.float32), 'w_qkv': jax.random.normal(k_wqkv, (3 * D_MODEL, D_MODEL), dtype=jnp.float32) * scale, 'b_qkv': jax.random.normal(k_bqkv, (3 * D_MODEL,), dtype=jnp.float32) * 0.01, 'w_out': jax.random.normal(k_wo, (D_MODEL, D_MODEL), dtype=jnp.float32) * scale, 'b_out': jax.random.normal(k_bo, (D_MODEL,), dtype=jnp.float32) * 0.01}
    _L0_attn_in = _L0_attn_setup()

    def _L0_ffn_setup():
        import jax, jax.numpy as jnp
        import numpy as np
        CAP_FACTOR = 1.25
        MIN_CAPACITY = 4

        def _capacity(num_tokens, num_experts):
            cap = int(np.floor(CAP_FACTOR * num_tokens / num_experts))
            cap += cap % 2
            return max(cap, MIN_CAPACITY)
        key = jax.random.key(seed)
        k1, k2, k3, k4 = jax.random.split(key, 4)
        B, S, H, I, E = (4, 256, 256, 1024, 8)
        inputs = jax.random.normal(k1, (B, S, H), dtype=jnp.float32)
        gate_weight = jax.random.normal(k2, (E, H), dtype=jnp.float32) * np.sqrt(0.1 / H)
        wi = jax.random.normal(k3, (E, H, I), dtype=jnp.float32) * np.sqrt(0.1 / H)
        wo = jax.random.normal(k4, (E, I, H), dtype=jnp.float32) * np.sqrt(0.1 / I)
        return {'inputs': inputs, 'gate_weight': gate_weight, 'wi': wi, 'wo': wo}
    _L0_ffn_in = _L0_ffn_setup()
    _L0_c = _w((lambda *s: np.random.randn(*s).astype(np.float32) * 0.05)(1, 256))
    _L0_wmod = _w((lambda *s: np.random.randn(*s).astype(np.float32) * 0.05)(256, 6 * 256) * 256 ** (-0.5))
    _d = {'L0_attn_x': _L0_attn_in['x'], 'L0_attn_w_qkv': _L0_attn_in['w_qkv'], 'L0_attn_b_qkv': _L0_attn_in['b_qkv'], 'L0_attn_w_out': _L0_attn_in['w_out'], 'L0_attn_b_out': _L0_attn_in['b_out'], 'L0_ffn_gate_weight': _L0_ffn_in['gate_weight'], 'L0_ffn_wi': _L0_ffn_in['wi'], 'L0_ffn_wo': _L0_ffn_in['wo'], 'L0_c': _L0_c, 'L0_wmod': _L0_wmod}
    _x0 = _d['L0_attn_x']
    _d['L0_attn_x'] = jax.random.normal(jax.random.fold_in(jax.random.key(seed), 1), (1, 2048, 256), dtype=_x0.dtype)
    del _x0
    return _d

def reference(L0_attn_x, L0_attn_w_qkv, L0_attn_b_qkv, L0_attn_w_out, L0_attn_b_out, L0_ffn_gate_weight, L0_ffn_wi, L0_ffn_wo, L0_c, L0_wmod):

    def _L0_attn_ref(x, w_qkv, b_qkv, w_out, b_out):
        import jax, jax.numpy as jnp
        import numpy as np
        import math
        D_MODEL = 256
        NUM_HEADS = 16
        HEAD_DIM = D_MODEL // NUM_HEADS
        B, S, D = x.shape
        H, Hd = (NUM_HEADS, HEAD_DIM)
        qkv = jnp.einsum('bsd,ed->bse', x, w_qkv) + b_qkv
        qkv = qkv.reshape(B, S, 3, H, Hd)
        q = jnp.transpose(qkv[:, :, 0], (0, 2, 1, 3))
        k = jnp.transpose(qkv[:, :, 1], (0, 2, 1, 3))
        v = jnp.transpose(qkv[:, :, 2], (0, 2, 1, 3))
        scores = jnp.einsum('bhqd,bhkd->bhqk', q, k) / math.sqrt(Hd)
        causal = jnp.triu(jnp.full((S, S), -jnp.inf, dtype=scores.dtype), k=1)
        scores = scores + causal[None, None]
        attn = jax.nn.softmax(scores, axis=-1)
        out = jnp.einsum('bhqk,bhkd->bhqd', attn, v)
        out = jnp.transpose(out, (0, 2, 1, 3)).reshape(B, S, D)
        return jnp.einsum('bsd,ed->bse', out, w_out) + b_out

    def _L0_ffn_ref(inputs, gate_weight, wi, wo):
        import jax, jax.numpy as jnp
        import numpy as np
        CAP_FACTOR = 1.25
        MIN_CAPACITY = 4

        def _capacity(num_tokens, num_experts):
            cap = int(np.floor(CAP_FACTOR * num_tokens / num_experts))
            cap += cap % 2
            return max(cap, MIN_CAPACITY)
        E, H = gate_weight.shape
        tokens = inputs.reshape(-1, H)
        T = tokens.shape[0]
        C = _capacity(T, E)
        gate_logits = tokens @ gate_weight.T
        gate = gate_logits.astype(jnp.float32)
        probs = jax.nn.softmax(gate, axis=-1)
        top1_idx = jnp.argmax(gate, axis=-1)
        mask = jax.nn.one_hot(top1_idx, E, dtype=jnp.int32)
        ranks = jnp.cumsum(mask, axis=0) - mask
        mask = mask * (ranks < C).astype(jnp.int32)
        rank1 = jnp.sum(mask * ranks, axis=-1)
        rank_oh = jax.nn.one_hot(rank1, C, dtype=inputs.dtype)
        weight = mask.astype(inputs.dtype) * probs.astype(inputs.dtype)
        combine_weights = weight[:, :, None] * rank_oh[:, None, :]
        sec_mask_f = (combine_weights != 0).astype(inputs.dtype)
        dispatch_data = jnp.einsum('tec,th->ech', sec_mask_f, tokens)
        h = jnp.einsum('ech,ehi->eci', dispatch_data, wi)
        h = jax.nn.gelu(h, approximate=False)
        expert_out = jnp.einsum('eci,eih->ech', h, wo)
        ans = jnp.einsum('tec,ech->th', combine_weights, expert_out)
        return ans.reshape(inputs.shape)
    x = L0_attn_x
    mod = (_silu(L0_c) @ L0_wmod).reshape(L0_c.shape[0], 6, 1, -1)
    sa, ca, ga, sb, cb, gb = (mod[:, 0], mod[:, 1], mod[:, 2], mod[:, 3], mod[:, 4], mod[:, 5])
    ga = (2 * (ga >= 0) - 1) * jnp.maximum(jnp.abs(ga), 0.25)
    gb = (2 * (gb >= 0) - 1) * jnp.maximum(jnp.abs(gb), 0.25)
    h = _layernorm(x, axis=-1) * (1 + ca) + sa
    x = x + ga * _L0_attn_ref(h, L0_attn_w_qkv, L0_attn_b_qkv, L0_attn_w_out, L0_attn_b_out)
    h = _layernorm(x, axis=-1) * (1 + cb) + sb
    x = x + gb * _L0_ffn_ref(h, L0_ffn_gate_weight, L0_ffn_wi, L0_ffn_wo)
    return x

_drawn_inputs = setup_inputs


def setup_inputs(seed=0):
    import zlib

    import numpy as np

    out = dict(_drawn_inputs(seed))
    spreads = {}
    factors = {'L0_attn_b_qkv': 8.0,
     'L0_attn_b_out': 8.0,
     'L0_ffn_gate_weight': 8.0,
     'L0_ffn_wi': 8.0,
     'L0_ffn_wo': 8.0}
    for name, (base, spread) in spreads.items():
        noise = np.random.default_rng([zlib.crc32(name.encode()), seed]).standard_normal(out[name].shape)
        drawn = base * np.exp(spread * noise) if base else spread * noise
        out[name] = jnp.asarray(drawn.astype(out[name].dtype))
    for name, factor in factors.items():
        out[name] = (out[name] * factor).astype(out[name].dtype)
    return out
```

```python
from contextlib import ExitStack

import concourse.bass as bass
from concourse import mybir

F32 = mybir.dt.float32
BF16 = mybir.dt.bfloat16
U32 = mybir.dt.uint32
ALU = mybir.AluOpType
ACT = mybir.ActivationFunctionType
AX = mybir.AxisListType

P = 128
D = 256
DT = D // P
S = 2048
NT = S // P
QB = 512
TB = QB // P
NB = S // QB
H = 16
HD = D // H
HG = 4
NG = H // HG
CT = 32
PARTS_Q = [0, 0, 1, 0, 1, 2]
PARTS_K = [0, 1, 0, 2, 1, 0]
KR = HD * len(PARTS_Q)
MR = 2 * HG
SCALE = HD ** -0.5
NEG = -3.0e38
E = 8
I = 1024
IT = I // P
CAP = 320
NS = E * CAP
ST = NS // P
EPS = 1e-5


def block_units():
    return [[(qt, h, c) for qt in range(TB) for h in range(HG) for c in range(b + 1)] for b in range(NB)]


def attention_plan():
    units = block_units()
    max_q = [(g, b, u) for g in range(NG) for b in range(NB) for u in range(len(units[b]))]
    plan = []
    done = 0
    t_vector = 0.0
    t_tensor = 0.0

    def emit_max():
        nonlocal done, t_vector, t_tensor
        g, b, u = max_q[done]
        qt, h, c = units[b][u]
        width = QB if c < b else P * (qt + 1)
        plan.append(("max", done, g, b, qt, h, c, width))
        done += 1
        t_vector += width / 0.96 + 66
        t_tensor += width / 2.4
        if u == len(units[b]) - 1:
            plan.append(("max_rows", g * NB + b))
            t_vector += 500

    def finish_max(n):
        while done < len(max_q) and max_q[done][0] * NB + max_q[done][1] <= n:
            emit_max()

    finish_max(0)
    t_vector = t_tensor = 0.0
    for n in range(NG * NB):
        g, b = divmod(n, NB)
        steps = (b + 1) * TB
        for kt in range(steps):
            if kt == steps - 3:
                finish_max(n + 1)
            for h in range(HG):
                plan.append(("scores", n, kt, h))
                width = QB - P * max(0, kt - b * TB)
                t_tensor = max(t_tensor + width / 2.4, t_vector - 3000)
                top = (g + 1, 1) if b >= 2 else (g, NB)
                if done < len(max_q) and t_vector < t_tensor + 1000 and max_q[done][:2] < top:
                    emit_max()
            plan.append(("values", n, kt))
            t_tensor += 4 * width / 2.4
            if b == 0 and g + 1 < NG:
                plan.append(("project", g + 1, kt))
                t_tensor += 1700
        plan.append(("heads_out", n))
    return plan


def layer(nc, x, w_qk, b_qk, w_v, w_o, b_rows, w_gate, w_in, w_down, c_col, w_mod, out):
    qk_parts = nc.dram_tensor("qk_parts", (2, 3, P, S), BF16, kind="Internal").ap()
    slot_rows = nc.dram_tensor("slot_rows", (NS, D), F32, kind="Internal").ap()
    slot_out = nc.dram_tensor("slot_out", (NS, D), F32, kind="Internal").ap()

    plan = attention_plan()
    misc_use = {}
    for ev in [("project", 0, b) for b in range(NB)] + plan:
        if ev[0] in ("max_rows", "heads_out", "project"):
            misc_use[ev] = len(misc_use)

    with ExitStack() as ctx:
        def sem(name):
            return ctx.enter_context(nc.semaphore(name))

        def sb(name, shape, dt):
            return ctx.enter_context(nc.sbuf_tensor(name, shape, dt))

        bank = [ctx.enter_context(nc.psum_tensor(f"bank{i}", [P, QB], F32)) for i in range(8)]
        MAX_BANKS, SCORE_BANKS, VALUE_BANK, MISC_BANK = (0, 1, 2), (3, 4, 5), 6, 7

        x_sb = sb("x_sb", [P, NT, D], F32)
        heads = sb("heads", [P, NT, D], F32)
        w_o_sb = sb("w_o_sb", [P, DT, D], F32)
        w_gate_sb = sb("w_gate_sb", [P, DT, E], F32)
        gates = sb("gates", [P, 2, D], F32)
        bias_row = sb("bias_row", [1, 2, D], F32)
        bias_all = sb("bias_all", [P, 2, D], F32)
        mod_col = sb("mod_col", [P, 4, DT], F32)
        ident = sb("ident", [P, P], F32)
        ident_b = sb("ident_b", [P, P], BF16)
        ones_f = sb("ones_f", [P, P], F32)
        stats = sb("stats", [P, NT, 6], F32)
        mean_var = sb("mean_var", [P, NT, 2], F32)
        root = sb("root", [P, 3, NT], F32)
        rstd = sb("rstd", [P, NT], F32)
        store = sb("store", [P, DT * S + NT * H * CT], F32)
        hT = store[:, 0:DT * S].rearrange("p (a s) -> p a s", a=DT)
        v_sb = store[:, DT * S:].rearrange("p (t h c) -> p t h c", t=NT, h=H)
        stacks = sb("stacks", [P, 2, 2, HG, S], BF16)
        probs = sb("probs", [P, 3, HG, QB], F32)
        early = probs[:, :, :, :].rearrange("p a b c -> p (a b c)")
        w_mod_sb = early[:, 0:DT * 6 * D].rearrange("p (t n) -> p t n", t=DT)
        xhat = early[:, DT * 6 * D:DT * 6 * D + TB * D].rearrange("p (t d) -> p t d", t=TB)
        silu_rep = early[:, DT * 6 * D + TB * D:DT * 6 * D + TB * D + DT * P].rearrange("p (t n) -> p t n", t=DT)
        w_qk_sb = sb("w_qk_sb", [P, DT, NG * P], F32)
        w_v_sb = sb("w_v_sb", [P, DT, D], F32)
        qk_sb = sb("qk_sb", [P, QB], F32)
        rest = sb("rest", [P, QB], F32)
        part = sb("part", [P, 3, QB], BF16)
        b_qk_sb = sb("b_qk_sb", [P, NG], F32)
        qk_scale = sb("qk_scale", [P, 1], F32)
        c_sb = sb("c_sb", [P, DT], F32)
        c_tmp = sb("c_tmp", [P, 3, DT], F32)
        silu = sb("silu", [P, DT], F32)
        sign = sb("sign", [P, 2, D], F32)
        causal = sb("causal", [P, QB], F32)
        masked = sb("masked", [P, 3, QB], BF16)
        head_sel = sb("head_sel", [P, HG], F32)
        chunk_max = sb("chunk_max", [P, 2, TB * HG, NB], F32)
        neg_max = sb("neg_max", [P, TB * HG], F32)
        max_part = sb("max_part", [P, 2, TB * HG, 2], BF16)
        o_sb = sb("o_sb", [P, 2, QB], F32)
        inv_sum = sb("inv_sum", [P, TB * HG], F32)
        stack_f = stacks[:, :, :, :, :].rearrange("p a b h s -> p (a b h s)").bitcast(F32)
        W_RING = 4
        w_ring = stack_f.rearrange("p (r n) -> p r n", r=W_RING)
        slots_sb = store[:, 0:ST * D].rearrange("p (t d) -> p t d", t=ST)
        slotT = store[:, ST * D:2 * ST * D].rearrange("p (t s) -> p t s", t=DT)
        spare = store[:, 2 * ST * D:]
        oT_sb = spare[:, 0:2 * D].rearrange("p (r n) -> p r n", r=2)
        h2T = spare[:, 2 * D:4 * D].rearrange("p (r n) -> p r n", r=2)
        down = spare[:, 0:2 * 3 * D].rearrange("p (r t d) -> p r t d", r=2, t=3)
        zeros = spare[:, 6 * D:8 * D]
        acts = early[:, 0:2 * IT * CAP].rearrange("p (r i c) -> p r i c", r=2, i=IT)
        logits = sb("logits", [P, NT, E], F32)
        expd = sb("expd", [P, NT, E], F32)
        top = sb("top", [P, NT], F32)
        prob = sb("prob", [P, NT], F32)
        onehot = sb("onehot", [P, NT, E], F32)
        onehot_b = sb("onehot_b", [P, NT, E], BF16)
        order = sb("order", [P, NT, E], F32)
        first_slot = sb("first_slot", [P, NT, E], F32)
        before = sb("before", [P, NT, E], F32)
        rank = sb("rank", [P, NT], F32)
        kept = sb("kept", [P, NT], F32)
        slot = sb("slot", [P, NT], F32)
        slot_to = sb("slot_to", [P, NT], U32)
        slot_from = sb("slot_from", [P, NT], U32)
        upper = sb("upper", [P, P], BF16)
        ones_b = sb("ones_b", [P, P], BF16)

        loaded_c = sem("loaded_c")
        loaded_mod = sem("loaded_mod")
        loaded_x = [sem(f"loaded_x{b}") for b in range(NB)]
        loaded_w = sem("loaded_w")
        pool_consts = sem("pool_consts")
        pool_chain = sem("pool_chain")
        v_zeroed = sem("v_zeroed")
        sel_ready = sem("sel_ready")
        c_exp = sem("c_exp")
        silu_ready = sem("silu_ready")
        mods_done = sem("mods_done")
        mods_read = sem("mods_read")
        dve_chain = sem("dve_chain")
        var_ready = sem("var_ready")
        root_ready = sem("root_ready")
        xhat_ready = sem("xhat_ready")
        xhat_turned = sem("xhat_turned")
        hT_ready = sem("hT_ready")
        v_done = sem("v_done")
        v_read = sem("v_read")
        x_biased = sem("x_biased")
        misc_done = sem("misc_done")
        misc_read_a = sem("misc_read_a")
        misc_read_v = sem("misc_read_v")
        qk_ready = sem("qk_ready")
        qk_split_v = sem("qk_split_v")
        qk_split_p = sem("qk_split_p")
        parts_stored = sem("parts_stored")
        stacked = sem("stacked")
        ones_rows = sem("ones_rows")
        max_scored = sem("max_scored")
        max_read = sem("max_read")
        max_parts = sem("max_parts")
        max_row0 = sem("max_row0")
        max_rows = sem("max_rows")
        scored = sem("scored")
        exp_done = sem("exp_done")
        diag_done = sem("diag_done")
        weighted = sem("weighted")
        o_read = sem("o_read")
        heads_ready = sem("heads_ready")
        zero_ready = sem("zero_ready")
        slots_zeroed = sem("slots_zeroed")
        heads_turned = sem("heads_turned")
        oT_ready = sem("oT_ready")
        projected = sem("projected")
        x1_ready = sem("x1_ready")
        xhat2_ready = sem("xhat2_ready")
        xhat2_turned = sem("xhat2_turned")
        h2T_ready = sem("h2T_ready")
        gated = sem("gated")
        exp_gate = sem("exp_gate")
        top_ready = sem("top_ready")
        onehot_ready = sem("onehot_ready")
        counted = sem("counted")
        slots_known = sem("slots_known")
        scattered = sem("scattered")
        slots_loaded = [sem(f"slots_loaded{i}") for i in range(ST // 4)]
        slots_turned = sem("slots_turned")
        slotT_ready = sem("slotT_ready")
        w_loaded = [sem(f"w_loaded{r}") for r in range(W_RING)]
        up_done = sem("up_done")
        gelu_done = sem("gelu_done")
        down_done = sem("down_done")
        down_read = sem("down_read")
        slot_stored = [sem(f"slot_stored{r}") for r in range(2)]
        fetched = sem("fetched")
        result_ready = sem("result_ready")
        stored = sem("stored")

        DIAG = [n * TB + j for n in range(NG * NB) for j in range(TB)]
        step_of = {}
        for n in range(NG * NB):
            for kt in range((n % NB + 1) * TB):
                step_of[n, kt] = len(step_of)
        last_step = [step_of[n, (n % NB + 1) * TB - 1] for n in range(NG * NB)]
        units_before = [0]
        for g in range(NG):
            for u in block_units():
                units_before.append(units_before[-1] + len(u))

        def misc_reads(index):
            kinds = [k[0] for k, i in misc_use.items() if i < index]
            return sum(k != "heads_out" for k in kinds), sum(k == "heads_out" for k in kinds)

        def stack(g, side):
            return stacks[:, g % 2, side, :, :]

        block = ctx.enter_context(nc.Block())

        def load_expert(eng, e):
            w = w_ring[:, e % W_RING, :]
            eng.dma_start(w[:, 0:DT * I].rearrange("p (t n) -> p t n", t=DT),
                          w_in[e].rearrange("(t p) n -> p t n", p=P)).then_inc(w_loaded[e % W_RING], 16)
            eng.dma_start(w[:, DT * I:].rearrange("p (t n) -> p t n", t=IT),
                          w_down[e].rearrange("(t p) n -> p t n", p=P)).then_inc(w_loaded[e % W_RING], 16)

        @block.sync
        def _(sp):
            sp.dma_start(c_sb[:, :], c_col).then_inc(loaded_c, 16)
            for b in range(NB):
                sp.dma_start(x_sb[:, b * TB:(b + 1) * TB, :],
                             x[b * QB:(b + 1) * QB, :].rearrange("(t p) d -> p t d", p=P)).then_inc(loaded_x[b], 16)
                if b == 0:
                    sp.dma_start(w_mod_sb[:, :, :], w_mod.rearrange("(t p) n -> p t n", p=P)).then_inc(loaded_mod, 16)
                    sp.dma_start(bias_row[:, :, :], b_rows.rearrange("(a t) d -> a t d", a=1)).then_inc(loaded_mod, 16)
            sp.dma_start(w_v_sb[:, :, :], w_v.rearrange("(t p) n -> p t n", p=P)).then_inc(loaded_w, 16)
            sp.dma_start(w_qk_sb[:, :, :], w_qk.rearrange("(t p) n -> p t n", p=P)).then_inc(loaded_w, 16)
            sp.dma_start(b_qk_sb[:, :], b_qk).then_inc(loaded_w, 16)
            sp.dma_start(w_o_sb[:, :, :], w_o.rearrange("(t p) n -> p t n", p=P)).then_inc(loaded_w, 16)
            sp.dma_start(w_gate_sb[:, :, :], w_gate.rearrange("(t p) n -> p t n", p=P)).then_inc(loaded_w, 16)
            for g in range(NG):
                for b in range(NB):
                    if g == 0:
                        sp.wait_ge(qk_split_v, b + 1)
                    else:
                        sp.wait_ge(qk_split_p, (g - 1) * NB + b + 1)
                    sp.dma_start(qk_parts[g % 2, :, :, b * QB:(b + 1) * QB].rearrange("a p s -> p a s"),
                                 part[:, :, :]).then_inc(parts_stored, 16)
                sp.wait_ge(parts_stored, 16 * NB * (g + 1))
                if g >= 2:
                    sp.wait_ge(scored, HG * (last_step[(g - 1) * NB - 1] + 1))
                for r in range(len(PARTS_Q)):
                    for side, parts in ((0, PARTS_Q), (1, PARTS_K)):
                        sp.dma_start(stack(g, side)[HD * r:HD * (r + 1)],
                                     qk_parts[g % 2, parts[r], side * P // 2:(side + 1) * P // 2, :]
                                     .rearrange("(h i) s -> i h s", i=HD)).then_inc(stacked, 16)
            sp.wait_ge(scored, HG * (last_step[-1] + 1))
            sp.wait_ge(max_scored, units_before[-1])
            for e in range(W_RING):
                load_expert(sp, e)
            sp.wait_ge(zero_ready, 1)
            for t in range(0, ST, 2):
                sp.dma_start(slot_rows[t * P:(t + 2) * P, :].rearrange("(t p) d -> p t d", p=P),
                             zeros.rearrange("p (t d) -> p t d", t=2)).then_inc(slots_zeroed, 16)
            sp.wait_ge(scattered, 16 * NT)
            for t in range(0, ST, 4):
                sp.dma_start(slots_sb[:, t:t + 4, :],
                             slot_rows[t * P:(t + 4) * P, :].rearrange("(t p) d -> p t d", p=P))\
                    .then_inc(slots_loaded[t // 4], 16)
            for e in range(E):
                sp.wait_ge(down_read, 3 * (e + 1))
                rows = slot_out[e * CAP:(e + 1) * CAP, :]
                sp.dma_start(rows[0:2 * P, :].rearrange("(t p) d -> p t d", p=P), down[:, e % 2, 0:2, :])\
                  .then_inc(slot_stored[e % 2], 16)
                sp.dma_start(rows[2 * P:CAP, :], down[0:CAP - 2 * P, e % 2, 2, :]).then_inc(slot_stored[e % 2], 16)
                if e + W_RING < E:
                    load_expert(sp, e + W_RING)
            for t in range(NT):
                sp.wait_ge(result_ready, t + 1)
                sp.dma_start(out[t * P:(t + 1) * P, :], x_sb[:, t, :]).then_inc(stored, 16)
            sp.wait_ge(stored, 16 * NT)

        def split_block(eng, ready, count, done):
            def link(ins):
                count[0] += 1
                ins.then_inc(ready, 1)
                eng.wait_ge(ready, count[0])
            link(eng.tensor_copy(part[:, 0, :], qk_sb[:, :]))
            link(eng.tensor_tensor(rest[:, :], qk_sb[:, :], part[:, 0, :], ALU.subtract))
            link(eng.tensor_copy(part[:, 1, :], rest[:, :]))
            eng.tensor_tensor(part[:, 2, :], rest[:, :], part[:, 1, :], ALU.subtract).then_inc(done, 1)

        @block.gpsimd
        def _(pool):
            chain = [0]

            def link(ins):
                chain[0] += 1
                ins.then_inc(pool_chain, 1)
                pool.wait_ge(pool_chain, chain[0])

            link(pool.memset(ident[:, :], 0.0))
            link(pool.affine_select(out=ident[:, :], in_=ident[:, :], compare_op=ALU.not_equal, fill=1.0, base=0,
                                    pattern=[[-1, P]], channel_multiplier=1))
            link(pool.memset(ones_f[:, :], 1.0))
            link(pool.tensor_copy(ident_b[:, :], ident[:, :]))
            link(pool.memset(ones_b[:, :], 1.0))
            link(pool.affine_select(out=upper[:, :], in_=ones_b[:, :], compare_op=ALU.is_gt, fill=0.0, base=0,
                                    pattern=[[1, P]], channel_multiplier=-1))
            link(pool.memset(qk_scale[0:P // 2, :], SCALE))
            link(pool.memset(qk_scale[P // 2:P, :], 1.0))
            link(pool.memset(causal[:, :], 0.0))
            link(pool.affine_select(out=causal[:, QB - P:QB], in_=causal[:, QB - P:QB], compare_op=ALU.is_ge,
                                    fill=NEG, base=0, pattern=[[-1, P]], channel_multiplier=1))
            link(pool.memset(head_sel[:, :], 1.0))
            rows = head_sel[KR:KR + MR, :]
            link(pool.affine_select(out=rows, in_=rows, compare_op=ALU.is_ge, fill=0.0, base=0,
                                    pattern=[[-2, HG]], channel_multiplier=1))
            link(pool.affine_select(out=rows, in_=rows, compare_op=ALU.is_ge, fill=0.0, base=1,
                                    pattern=[[2, HG]], channel_multiplier=-1))
            for e in range(E):
                pool.memset(order[:, :, e], float(E - e))
                last = pool.memset(first_slot[:, :, e], float(CAP * e))
            link(last)
            pool.memset(ones_f[0:1, 0:1], 1.0).then_inc(pool_consts, 1)
            link(pool.memset(v_sb[:, :, :, :], 0.0))
            pool.memset(v_sb[:, :, :, HD:HD + 1], 1.0).then_inc(v_zeroed, 1)
            pool.wait_ge(mods_read, 4)
            link(pool.tensor_tensor(sign[:, 0, :], gates[:, 0, :], bias_all[:, 1, :], ALU.mult))
            for t in range(NT):
                pool.wait_ge(xhat_ready, t + 1)
                last = pool.tensor_tensor(x_sb[:, t, :], x_sb[:, t, :], sign[:, 0, :], ALU.add)
            last.then_inc(x_biased, 1)

            splits = diags = 0
            for ev in plan:
                if ev[0] == "project":
                    pool.wait_ge(qk_ready, NB + splits + 1)
                    pool.wait_ge(parts_stored, 16 * (NB + splits))
                    for i, (o, a, b_) in enumerate((
                            (part[:, 0, :], qk_sb[:, :], None), (rest[:, :], qk_sb[:, :], part[:, 0, :]),
                            (part[:, 1, :], rest[:, :], None), (part[:, 2, :], rest[:, :], part[:, 1, :]))):
                        ins = pool.tensor_copy(o, a) if b_ is None else pool.tensor_tensor(o, a, b_, ALU.subtract)
                        if i < 3:
                            link(ins)
                        else:
                            ins.then_inc(qk_split_p, 1)
                    splits += 1
                if ev[0] == "max_rows":
                    n = ev[1]
                    g, b = divmod(n, NB)
                    rows = stack(g, 0)[KR:KR + MR, :, b * QB:(b + 1) * QB]
                    pool.wait_ge(max_row0, n + 1)
                    pool.wait_ge(x_biased, 1)
                    if diags:
                        pool.wait_ge(diag_done, diags)
                    if splits:
                        pool.wait_ge(qk_split_p, splits)
                    pool.tensor_copy(rows[:, 1:HG, :], rows[:, 0:1, :].broadcast_to([MR, HG - 1, QB]))\
                        .then_inc(max_rows, 1)
                    pool.wait_ge(max_rows, n + 1)
                if ev[0] == "scores" and ev[3] == HG - 1:
                    _, n, kt, h = ev
                    j = kt - (n % NB) * TB
                    if j >= 0:
                        s = step_of[n, kt]
                        pool.wait_ge(exp_done, HG * (s + 1))
                        d = probs[:, s % 3, :, 0:P]
                        pool.affine_select(out=d, in_=d, compare_op=ALU.is_ge, fill=0.0, base=0,
                                           pattern=[[0, HG], [1, P]], channel_multiplier=-1).then_inc(diag_done, 1)
                        diags += 1
            pool.wait_ge(weighted, last_step[-1] + 1)
            pool.memset(zeros, 0.0).then_inc(zero_ready, 1)
            pool.wait_ge(slots_zeroed, 16 * ST // 2)
            pool.wait_ge(slots_known, 1)
            for t in range(NT):
                pool.indirect_dma_start(out=slot_rows, out_offset=bass.IndirectOffsetOnAxis(ap=slot_to[:, t:t + 1], axis=0),
                                        in_=heads[:, t, :], in_offset=None, bounds_check=NS - 1,
                                        oob_is_err=False).then_inc(scattered, 16)
            pool.wait_ge(scattered, 16 * NT)
            pool.wait_ge(slot_stored[0], 16 * E)
            pool.wait_ge(slot_stored[1], 16 * E)
            for t in range(NT):
                pool.indirect_dma_start(out=heads[:, t, :], out_offset=None, in_=slot_out,
                                        in_offset=bass.IndirectOffsetOnAxis(ap=slot_from[:, t:t + 1], axis=0))\
                    .then_inc(fetched, 16)

        @block.scalar
        def _(act):
            act.wait_ge(loaded_c, 16)
            act.activation(c_tmp[:, 0, :], c_sb[:, :], ACT.Exp, scale=-1.0).then_inc(c_exp, 1)
            for b in range(NB):
                act.wait_ge(var_ready, b + 1)
                act.activation(root[:, 0, b * TB:(b + 1) * TB], root[:, 1, b * TB:(b + 1) * TB], ACT.Sqrt)\
                    .then_inc(root_ready, 1)
            def read_projection(g, b):
                n = g * NB + b
                act.wait_ge(misc_done, misc_use["project", g, b] + 1)
                if n >= 1:
                    if n <= NB:
                        act.wait_ge(qk_split_v, n)
                    else:
                        act.wait_ge(qk_split_p, n - NB)
                act.activation(qk_sb[:, :], bank[MISC_BANK][:, :], ACT.Identity, bias=b_qk_sb[:, g:g + 1],
                               scale=qk_scale[:, 0:1]).then_inc(misc_read_a, 1)
                act.wait_ge(misc_read_a, misc_reads(misc_use["project", g, b])[0] + 1)
                act.copy(c_tmp[0:1, 1, 0:1], c_tmp[0:1, 0, 0:1]).then_inc(qk_ready, 1)

            act.wait_ge(mods_read, 4)
            for b in range(NB):
                for ft in range(DT):
                    act.wait_ge(xhat_turned, b * DT + ft + 1)
                    act.activation(hT[:, ft, b * QB:(b + 1) * QB], bank[ft][:, :], ACT.Identity,
                                   bias=mod_col[:, 0, ft:ft + 1], scale=mod_col[:, 1, ft:ft + 1]).then_inc(hT_ready, 1)
                if b == 0:
                    act.wait_ge(silu_ready, 2)
                read_projection(0, b)
            for ev in plan:
                if ev[0] == "project":
                    read_projection(ev[1], ev[2])
                if ev[0] == "max_rows":
                    n = ev[1]
                    g, b = divmod(n, NB)
                    act.wait_ge(misc_done, misc_use[ev] + 1)
                    act.copy(stack(g, 0)[KR:KR + MR, 0, b * QB:(b + 1) * QB],
                             bank[MISC_BANK][:, :].bitcast(BF16)[0:MR, 0:QB]).then_inc(misc_read_a, 1)
                    act.wait_ge(misc_read_a, misc_reads(misc_use[ev])[0] + 1)
                    act.copy(c_tmp[0:1, 1, 0:1], c_tmp[0:1, 0, 0:1]).then_inc(max_row0, 1)
                if ev[0] == "scores":
                    _, n, kt, h = ev
                    s = step_of[n, kt]
                    u = HG * s + h
                    width = QB - P * max(0, kt - (n % NB) * TB)
                    act.wait_ge(scored, u + 1)
                    if h == 0 and s >= 3:
                        act.wait_ge(weighted, s - 2)
                    act.activation(probs[:, s % 3, h, 0:width], bank[SCORE_BANKS[u % 3]][:, 0:width], ACT.Exp)\
                        .then_inc(exp_done, 1)
                if ev[0] == "heads_out":
                    n = ev[1]
                    act.wait_ge(weighted, last_step[n] + 1)
                    if n >= 2:
                        act.wait_ge(misc_done, misc_use["heads_out", n - 2] + 1)
                    act.copy(o_sb[:, n % 2, :], bank[VALUE_BANK][:, :]).then_inc(o_read, 1)

            for t in range(NT):
                act.wait_ge(heads_turned, t + 1)
                if t >= 2:
                    act.wait_ge(projected, t - 1)
                act.copy(oT_sb[:, t % 2, :], bank[t % 2][:, 0:D]).then_inc(oT_ready, 1)
            for b in range(NB):
                act.wait_ge(var_ready, NB + b + 1)
                act.activation(root[:, 0, b * TB:(b + 1) * TB], root[:, 1, b * TB:(b + 1) * TB], ACT.Sqrt)\
                    .then_inc(root_ready, 1)
            for t in range(NT):
                act.wait_ge(xhat2_turned, t + 1)
                if t >= 2:
                    act.wait_ge(gated, t - 1)
                for ft in range(DT):
                    act.activation(h2T[:, t % 2, ft * P:(ft + 1) * P], bank[4 + t % 2][:, ft * P:(ft + 1) * P],
                                   ACT.Identity, bias=mod_col[:, 2, ft:ft + 1],
                                   scale=mod_col[:, 3, ft:ft + 1]).then_inc(h2T_ready, 1)
            act.wait_ge(top_ready, 1)
            act.activation(expd[:, :, :], expd[:, :, :], ACT.Exp).then_inc(exp_gate, 1)
            for t in range(ST // 2):
                act.wait_ge(slots_turned, t + 1)
                for ft in range(DT):
                    act.activation(slotT[:, ft, t * 2 * P:(t + 1) * 2 * P], bank[t % 2][:, ft * 2 * P:(ft + 1) * 2 * P],
                                   ACT.Identity, bias=mod_col[:, 2, ft:ft + 1],
                                   scale=mod_col[:, 3, ft:ft + 1]).then_inc(slotT_ready, 1)
            for e in range(E):
                for it in range(IT):
                    k = e * IT + it
                    act.wait_ge(up_done, k + 1)
                    if e >= 2 and it == 0:
                        act.wait_ge(down_done, 3 * (e - 1))
                    act.activation(acts[:, e % 2, it, :], bank[2 + k % 3][:, 0:CAP], ACT.Gelu).then_inc(gelu_done, 1)

        @block.vector
        def _(dve):
            chain = [0]

            def link(ins):
                chain[0] += 1
                ins.then_inc(dve_chain, 1)
                dve.wait_ge(dve_chain, chain[0])

            dve.wait_ge(c_exp, 1)
            link(dve.tensor_scalar(c_tmp[:, 1, :], c_tmp[:, 0, :], 1.0, None, ALU.add))
            link(dve.reciprocal(c_tmp[:, 2, :], c_tmp[:, 1, :]))
            dve.tensor_tensor(silu[:, :], c_sb[:, :], c_tmp[:, 2, :], ALU.mult).then_inc(silu_ready, 1)
            dve.wait_ge(pool_consts, 1)
            dve.wait_ge(silu_ready, 1)
            for ft in range(DT):
                last = dve.tensor_scalar(silu_rep[:, ft, :], ones_f[:, :], silu[:, ft:ft + 1], None, ALU.mult)
            dve.wait_ge(loaded_w, 80)
            link(last)
            dve.tensor_scalar(b_qk_sb[:, :], b_qk_sb[:, :], qk_scale[:, 0:1], None, ALU.mult).then_inc(silu_ready, 1)

            def variances(src, b):
                for t in range(b * TB, (b + 1) * TB):
                    last = dve.bn_stats(stats[:, t, :], src[:, t, :])
                link(last)
                for t in range(b * TB, (b + 1) * TB):
                    last = dve.bn_aggr(mean_var[:, t, :], stats[:, t, :])
                link(last)
                dve.tensor_scalar(root[:, 1, b * TB:(b + 1) * TB], mean_var[:, b * TB:(b + 1) * TB, 1], EPS, None,
                                  ALU.add).then_inc(var_ready, 1)

            def inverse_root(b, waits):
                ts = slice(b * TB, (b + 1) * TB)
                dve.wait_ge(root_ready, waits)
                link(dve.reciprocal(root[:, 2, ts], root[:, 0, ts]))
                link(dve.tensor_tensor(root[:, 2, ts], root[:, 2, ts], root[:, 1, ts], ALU.mult))
                link(dve.tensor_tensor(root[:, 2, ts], root[:, 2, ts], root[:, 0, ts], ALU.add))
                link(dve.tensor_scalar(root[:, 2, ts], root[:, 2, ts], 0.5, None, ALU.mult))
                link(dve.reciprocal(rstd[:, ts], root[:, 2, ts]))

            for b in range(NB):
                dve.wait_ge(loaded_x[b], 16)
                variances(x_sb, b)
            def values_and_split(b):
                if b == 0:
                    dve.wait_ge(v_zeroed, 1)
                for t in range(b * TB, (b + 1) * TB):
                    dve.wait_ge(v_done, t + 1)
                    dve.tensor_tensor(v_sb[:, t, :, 0:HD], bank[2 + t % 2][:, 0:D].rearrange("p (h i) -> p h i", h=H),
                                      bias_all[:, 0, :].rearrange("p (h i) -> p h i", h=H), ALU.add).then_inc(v_read, 1)
                dve.wait_ge(qk_ready, b + 1)
                if b >= 1:
                    dve.wait_ge(parts_stored, 16 * b)
                split_block(dve, dve_chain, chain, qk_split_v)

            for b in range(NB):
                inverse_root(b, b + 1)
                for t in range(b * TB, (b + 1) * TB):
                    if b >= 1:
                        dve.wait_ge(xhat_turned, b * DT)
                    dve.tensor_scalar(xhat[:, t % 4, :], x_sb[:, t, :], mean_var[:, t, 0:1], rstd[:, t:t + 1],
                                      ALU.subtract, ALU.mult).then_inc(xhat_ready, 1)
                if b == 0:
                    dve.wait_ge(mods_done, 1)
                    mods = bank[4][:, 0:4 * DT].rearrange("p (m t) -> p m t", m=4)
                    for m in range(4):
                        last = dve.tensor_scalar(mod_col[:, m, :], mods[:, m, :], float(m % 2), None, ALU.add)
                    last.then_inc(mods_read, 1)
                    g2 = gates[:, :, :].rearrange("p a d -> p (a d)")
                    s2 = sign[:, :, :].rearrange("p a d -> p (a d)")
                    dve.tensor_copy(bias_all[:, :, :].rearrange("p a d -> p (a d)"), bank[6][:, :]).then_inc(mods_read, 1)
                    link(dve.tensor_scalar(s2, bank[5][:, :], 0.0, 2.0, ALU.is_ge, ALU.mult))
                    link(dve.tensor_scalar(s2, s2, -1.0, None, ALU.add))
                    link(dve.tensor_tensor(g2, bank[5][:, :], s2, ALU.mult))
                    dve.tensor_scalar(g2, g2, 0.25, None, ALU.max).then_inc(mods_read, 1)
                    dve.wait_ge(mods_read, 3)
                    dve.tensor_tensor(g2, g2, s2, ALU.mult).then_inc(mods_read, 1)
                    dve.wait_ge(pool_consts, 1)
                    for par in range(2):
                        for h in range(HG):
                            last = dve.memset(stacks[KR:KR + MR, par, 1, h, :], 1.0)
                    link(last)
                    for par in range(2):
                        for h in range(HG):
                            last = dve.tensor_scalar(stacks[KR:KR + MR, par, 1, h, :], stacks[KR:KR + MR, par, 1, h, :],
                                                     head_sel[KR:KR + MR, h:h + 1], None, ALU.mult)
                    last.then_inc(ones_rows, 1)
                else:
                    values_and_split(b - 1)
            values_and_split(NB - 1)

            for ev in plan:
                if ev[0] == "max":
                    _, u, g, b, qt, h, c, width = ev
                    n = g * NB + b
                    src = bank[MAX_BANKS[u % 3]]
                    to = chunk_max[:, n % 2, qt * HG + h, c:c + 1]
                    dve.wait_ge(max_scored, u + 1)
                    if c < b:
                        dve.tensor_reduce(to, src[:, 0:QB], AX.X, ALU.max).then_inc(max_read, 1)
                    else:
                        if u >= 3:
                            dve.wait_ge(max_read, u - 2)
                        dve.tensor_tensor_reduce(out=masked[:, u % 3, 0:width], in0=src[:, 0:width],
                                                 in1=causal[:, QB - width:QB], scale=1.0, scalar=NEG, op0=ALU.add,
                                                 op1=ALU.max, accum_out=to).then_inc(max_read, 1)
                if ev[0] == "max_rows":
                    n = ev[1]
                    b = n % NB
                    dve.wait_ge(max_read, units_before[n + 1])
                    link(dve.tensor_reduce(neg_max[:, :], chunk_max[:, n % 2, :, 0:b + 1], AX.X, ALU.max, negate=True))
                    if n >= 2:
                        dve.wait_ge(misc_done, misc_use["max_rows", n - 2] + 1)
                    link(dve.tensor_copy(max_part[:, n % 2, :, 0], neg_max[:, :]))
                    dve.tensor_tensor(max_part[:, n % 2, :, 1], neg_max[:, :], max_part[:, n % 2, :, 0], ALU.subtract)\
                        .then_inc(max_parts, 1)
                if ev[0] == "heads_out":
                    n = ev[1]
                    g, b = divmod(n, NB)
                    dve.wait_ge(misc_done, misc_use[ev] + 1)
                    o = bank[MISC_BANK][:, :].rearrange("p (t h c) -> p t h c", t=TB, h=HG)
                    inv = inv_sum[:, :].rearrange("p (t h) -> p t h", t=TB)
                    link(dve.reciprocal(inv, o[:, :, :, HD]))
                    to = heads[:, b * TB:(b + 1) * TB, g * HG * HD:(g + 1) * HG * HD]
                    dve.tensor_tensor(to.rearrange("p t (h i) -> p t h i", h=HG), o[:, :, :, 0:HD],
                                      inv.rearrange("p t (h i) -> p t h i", i=1).broadcast_to([P, TB, HG, HD]), ALU.mult)\
                        .then_inc(misc_read_v, 1)

            dve.wait_ge(x_biased, 1)
            for b in range(NB):
                for t in range(b * TB, (b + 1) * TB):
                    dve.wait_ge(projected, t + 1)
                    link(dve.tensor_tensor(sign[:, t % 2, :], bank[2 + t % 2][:, 0:D], gates[:, 0, :], ALU.mult))
                    dve.tensor_tensor(x_sb[:, t, :], x_sb[:, t, :], sign[:, t % 2, :], ALU.add).then_inc(x1_ready, 1)
                dve.wait_ge(x1_ready, (b + 1) * TB)
                variances(x_sb, b)
            for b in range(NB):
                inverse_root(b, NB + b + 1)
                dve.wait_ge(heads_turned, (b + 1) * TB)
                for t in range(b * TB, (b + 1) * TB):
                    dve.tensor_scalar(heads[:, t, :], x_sb[:, t, :], mean_var[:, t, 0:1], rstd[:, t:t + 1],
                                      ALU.subtract, ALU.mult).then_inc(xhat2_ready, 1)

            dve.wait_ge(gated, NT)

            def wide(a):
                return a.rearrange("p (t e) -> p t e", e=1).broadcast_to([P, NT, E])
            link(dve.tensor_copy(logits[:, :, :], bank[6][:, 0:NT * E].rearrange("p (t e) -> p t e", e=E)))
            link(dve.tensor_reduce(top[:, :], logits[:, :, :], AX.X, ALU.max))
            dve.tensor_tensor(expd[:, :, :], logits[:, :, :], wide(top[:, :]), ALU.subtract).then_inc(top_ready, 1)
            link(dve.tensor_tensor(onehot[:, :, :], logits[:, :, :], wide(top[:, :]), ALU.is_ge))
            link(dve.tensor_tensor(onehot[:, :, :], onehot[:, :, :], order[:, :, :], ALU.mult))
            link(dve.tensor_reduce(top[:, :], onehot[:, :, :], AX.X, ALU.max))
            link(dve.tensor_tensor(onehot[:, :, :], onehot[:, :, :], wide(top[:, :]), ALU.is_equal))
            dve.tensor_copy(onehot_b[:, :, :], onehot[:, :, :]).then_inc(onehot_ready, 1)
            dve.wait_ge(exp_gate, 1)
            link(dve.tensor_reduce(prob[:, :], expd[:, :, :], AX.X, ALU.add))
            link(dve.reciprocal(prob[:, :], prob[:, :]))
            dve.wait_ge(counted, 1)
            link(dve.tensor_copy(before[:, :, :], bank[1][:, 0:NT * E].rearrange("p (t e) -> p t e", e=E)))
            link(dve.memset(logits[:, 0, :], 0.0))
            for t in range(1, NT):
                link(dve.tensor_tensor(logits[:, t, :], logits[:, t - 1, :], before[:, t - 1, :], ALU.add))
            link(dve.tensor_tensor(before[:, :, :], bank[0][:, 0:NT * E].rearrange("p (t e) -> p t e", e=E),
                                   logits[:, :, :], ALU.add))
            link(dve.tensor_tensor(before[:, :, :], before[:, :, :], onehot[:, :, :], ALU.mult))
            link(dve.tensor_reduce(rank[:, :], before[:, :, :], AX.X, ALU.add))
            link(dve.tensor_scalar(kept[:, :], rank[:, :], float(CAP), None, ALU.is_lt))
            link(dve.tensor_tensor(before[:, :, :], onehot[:, :, :], first_slot[:, :, :], ALU.mult))
            link(dve.tensor_reduce(slot[:, :], before[:, :, :], AX.X, ALU.add))
            link(dve.tensor_tensor(slot[:, :], slot[:, :], rank[:, :], ALU.add))
            link(dve.tensor_tensor(slot[:, :], slot[:, :], kept[:, :], ALU.mult))
            link(dve.tensor_copy(slot_from[:, :], slot[:, :]))
            link(dve.tensor_scalar(top[:, :], kept[:, :], -float(NS), float(NS), ALU.mult, ALU.add))
            link(dve.tensor_tensor(top[:, :], top[:, :], slot[:, :], ALU.add))
            link(dve.tensor_tensor(prob[:, :], prob[:, :], kept[:, :], ALU.mult))
            dve.tensor_copy(slot_to[:, :], top[:, :]).then_inc(slots_known, 1)

            for e in range(E):
                if e >= 2:
                    dve.wait_ge(slot_stored[e % 2], 32 * (e // 2))
                for st in range(3):
                    k = 3 * e + st
                    rows = min(P, CAP - st * P)
                    dve.wait_ge(down_done, k + 1)
                    dve.tensor_copy(down[0:rows, e % 2, st, :], bank[5 + k % 3][0:rows, 0:D]).then_inc(down_read, 1)
            dve.wait_ge(fetched, 16 * NT)
            for t in range(NT):
                link(dve.scalar_tensor_tensor(out=heads[:, t, :], in0=heads[:, t, :], scalar=prob[:, t:t + 1],
                                              in1=gates[:, 1, :], op0=ALU.mult, op1=ALU.mult))
                dve.tensor_tensor(x_sb[:, t, :], x_sb[:, t, :], heads[:, t, :], ALU.add).then_inc(result_ready, 1)

        @block.tensor
        def _(pe):
            pe.wait_ge(pool_consts, 1)
            pe.wait_ge(loaded_mod, 32)
            pe.wait_ge(silu_ready, 2)
            for j, m in enumerate((0, 1, 3, 4)):
                for ft in range(DT):
                    for k in range(DT):
                        pe.matmul(bank[4][:, j * DT + ft:j * DT + ft + 1],
                                  w_mod_sb[:, k, m * D + ft * P:m * D + (ft + 1) * P], silu[:, k:k + 1],
                                  start=(k == 0), stop=(k == DT - 1))
            for j, m in enumerate((2, 5)):
                for k in range(DT):
                    pe.matmul(bank[5][:, j * D:(j + 1) * D], silu_rep[:, k, :], w_mod_sb[:, k, m * D:(m + 1) * D],
                              start=(k == 0), stop=(k == DT - 1))
            pe.matmul(bank[6][:, :], ones_f[0:1, :], bias_row[:, :, :].rearrange("a t d -> a (t d)"),
                      start=True, stop=True).then_inc(mods_done, 1)

            def project(g, b):
                use = misc_use["project", g, b]
                a, v = misc_reads(use)
                if use >= 1:
                    pe.wait_ge(misc_read_a, a)
                    if v:
                        pe.wait_ge(misc_read_v, v)
                for k in range(DT):
                    mm = pe.matmul(bank[MISC_BANK][:, :], w_qk_sb[:, k, g * P:(g + 1) * P],
                                   hT[:, k, b * QB:(b + 1) * QB], start=(k == 0), stop=(k == DT - 1))
                mm.then_inc(misc_done, 1)

            for b in range(NB):
                pe.wait_ge(xhat_ready, (b + 1) * TB)
                if b >= 1:
                    pe.wait_ge(hT_ready, b * DT)
                for ft in range(DT):
                    for t in range(TB):
                        mm = pe.transpose(bank[ft][:, t * P:(t + 1) * P], xhat[:, t, ft * P:(ft + 1) * P], ident[:, :])
                    mm.then_inc(xhat_turned, 1)
                pe.wait_ge(hT_ready, (b + 1) * DT)
                pe.wait_ge(loaded_w, 80)
                project(0, b)
                for t in range(b * TB, (b + 1) * TB):
                    if t >= 2:
                        pe.wait_ge(v_read, t - 1)
                    for k in range(DT):
                        mm = pe.matmul(bank[2 + t % 2][:, 0:D], hT[:, k, t * P:(t + 1) * P], w_v_sb[:, k, :],
                                       start=(k == 0), stop=(k == DT - 1))
                    mm.then_inc(v_done, 1)

            def misc_free(ev):
                a, v = misc_reads(misc_use[ev])
                pe.wait_ge(misc_read_a, a)
                if v:
                    pe.wait_ge(misc_read_v, v)

            def turn_heads(n):
                pe.wait_ge(o_read, n + 1)
                misc_free(("heads_out", n))
                for t in range(TB):
                    mm = pe.transpose(bank[MISC_BANK][:, t * P:(t + 1) * P], o_sb[:, n % 2, t * P:(t + 1) * P], ident[:, :])
                mm.then_inc(misc_done, 1)

            def weigh_values(n, kt):
                s = step_of[n, kt]
                j = kt - (n % NB) * TB
                if j >= 0:
                    pe.wait_ge(diag_done, n * TB + j + 1)
                else:
                    pe.wait_ge(exp_done, HG * (s + 1))
                if kt == 0 and n >= 1:
                    pe.wait_ge(o_read, n)
                lo = P * max(0, j)
                g = n // NB
                for h in range(HG):
                    mm = pe.matmul(bank[VALUE_BANK][CT * h:CT * (h + 1), lo:QB], v_sb[:, kt, g * HG + h, :],
                                   probs[:, s % 3, h, 0:QB - lo], start=(kt == 0), stop=(j == TB - 1),
                                   skip_group_check=True)
                mm.then_inc(weighted, 1)

            pe.wait_ge(ones_rows, 1)
            pe.wait_ge(hT_ready, NB * DT)
            pe.wait_ge(v_read, NT)
            pe.wait_ge(mods_read, 4)
            pending = None
            for ev in plan:
                if ev[0] == "max":
                    _, u, g, b, qt, h, c, width = ev
                    if (b, qt, h, c) == (0, 0, 0, 0):
                        pe.wait_ge(stacked, 16 * 2 * len(PARTS_Q) * (g + 1))
                    if u >= 3:
                        pe.wait_ge(max_read, u - 2)
                    q0 = b * QB + qt * P
                    pe.matmul(bank[MAX_BANKS[u % 3]][:, 0:width], stack(g, 0)[0:KR, h, q0:q0 + P],
                              stack(g, 1)[0:KR, h, c * QB:c * QB + width], start=True, stop=True).then_inc(max_scored, 1)
                if ev[0] == "max_rows":
                    n = ev[1]
                    pe.wait_ge(max_parts, n + 1)
                    misc_free(ev)
                    for t in range(TB):
                        mm = pe.transpose(bank[MISC_BANK][:, :].bitcast(BF16)[0:MR, t * P:(t + 1) * P],
                                          max_part[:, n % 2, t * HG:(t + 1) * HG, :].rearrange("p h a -> p (h a)"),
                                          ident_b[:, :])
                    mm.then_inc(misc_done, 1)
                if ev[0] == "project":
                    misc_free(ev)
                    project(ev[1], ev[2])
                if ev[0] == "scores":
                    _, n, kt, h = ev
                    g, b = divmod(n, NB)
                    u = HG * step_of[n, kt] + h
                    lo = P * max(0, kt - b * TB)
                    if kt == 0 and h == 0:
                        pe.wait_ge(max_rows, n + 1)
                    if u >= 3:
                        pe.wait_ge(exp_done, u - 2)
                    pe.matmul(bank[SCORE_BANKS[u % 3]][:, 0:QB - lo], stack(g, 1)[0:KR + MR, h, kt * P:(kt + 1) * P],
                              stack(g, 0)[0:KR + MR, h, b * QB + lo:(b + 1) * QB], start=True, stop=True)\
                        .then_inc(scored, 1)
                if ev[0] == "values":
                    if pending:
                        weigh_values(*pending)
                    pending = ev[1:]
                if ev[0] == "heads_out":
                    weigh_values(*pending)
                    pending = None
                    turn_heads(ev[1])

            pe.wait_ge(misc_read_v, NG * NB)

            def turn_tile(t):
                if t >= 2:
                    pe.wait_ge(oT_ready, t - 1)
                for ft in range(DT):
                    mm = pe.transpose(bank[t % 2][:, ft * P:(ft + 1) * P], heads[:, t, ft * P:(ft + 1) * P], ident[:, :])
                mm.then_inc(heads_turned, 1)
            turn_tile(0)
            for t in range(NT):
                if t + 1 < NT:
                    turn_tile(t + 1)
                pe.wait_ge(oT_ready, t + 1)
                if t >= 2:
                    pe.wait_ge(x1_ready, t - 1)
                for k in range(DT):
                    mm = pe.matmul(bank[2 + t % 2][:, 0:D], oT_sb[:, t % 2, k * P:(k + 1) * P], w_o_sb[:, k, :],
                                   start=(k == 0), stop=(k == DT - 1))
                mm.then_inc(projected, 1)

            def turn_normal(t):
                pe.wait_ge(xhat2_ready, t + 1)
                if t >= 2:
                    pe.wait_ge(h2T_ready, DT * (t - 1))
                for ft in range(DT):
                    mm = pe.transpose(bank[4 + t % 2][:, ft * P:(ft + 1) * P], heads[:, t, ft * P:(ft + 1) * P], ident[:, :])
                mm.then_inc(xhat2_turned, 1)
            turn_normal(0)
            for t in range(NT):
                if t + 1 < NT:
                    turn_normal(t + 1)
                pe.wait_ge(h2T_ready, DT * (t + 1))
                for k in range(DT):
                    mm = pe.matmul(bank[6][:, t * E:(t + 1) * E], h2T[:, t % 2, k * P:(k + 1) * P], w_gate_sb[:, k, :],
                                   start=(k == 0), stop=(k == DT - 1))
                mm.then_inc(gated, 1)
            pe.wait_ge(onehot_ready, 1)
            chosen = onehot_b[:, :, :].rearrange("p t e -> p (t e)")
            pe.matmul(bank[0][:, 0:NT * E], upper[:, :], chosen, start=True, stop=True)
            pe.matmul(bank[1][:, 0:NT * E], ones_b[:, :], chosen, start=True, stop=True).then_inc(counted, 1)
            pe.wait_ge(slots_known, 1)

            for t in range(ST // 2):
                if t % 2 == 0:
                    pe.wait_ge(slots_loaded[t // 2], 16)
                if t >= 2:
                    pe.wait_ge(slotT_ready, DT * (t - 1))
                for ft in range(DT):
                    for j in range(2):
                        mm = pe.transpose(bank[t % 2][:, (2 * ft + j) * P:(2 * ft + j + 1) * P],
                                          slots_sb[:, 2 * t + j, ft * P:(ft + 1) * P], ident[:, :])
                mm.then_inc(slots_turned, 1)

            pe.wait_ge(slotT_ready, DT * ST // 2)

            def up(e):
                pe.wait_ge(w_loaded[e % W_RING], 32 * (e // W_RING + 1))
                w = w_ring[:, e % W_RING, 0:DT * I].rearrange("p (t n) -> p t n", t=DT)
                for it in range(IT):
                    n = e * IT + it
                    if n >= 3:
                        pe.wait_ge(gelu_done, n - 2)
                    for k in range(DT):
                        mm = pe.matmul(bank[2 + n % 3][:, 0:CAP], w[:, k, it * P:(it + 1) * P],
                                       slotT[:, k, e * CAP:(e + 1) * CAP], start=(k == 0), stop=(k == DT - 1))
                    mm.then_inc(up_done, 1)

            def down_to(e):
                w = w_ring[:, e % W_RING, DT * I:].rearrange("p (t n) -> p t n", t=IT)
                pe.wait_ge(gelu_done, IT * (e + 1))
                for st in range(3):
                    n = 3 * e + st
                    rows = min(P, CAP - st * P)
                    if n >= 3:
                        pe.wait_ge(down_read, n - 2)
                    for it in range(IT):
                        mm = pe.matmul(bank[5 + n % 3][0:rows, 0:D], acts[:, e % 2, it, st * P:st * P + rows],
                                       w[:, it, :], start=(it == 0), stop=(it == IT - 1))
                    mm.then_inc(down_done, 1)
            up(0)
            for e in range(E):
                if e + 1 < E:
                    up(e + 1)
                down_to(e)


def kernel(L0_attn_x, L0_attn_w_qkv, L0_attn_b_qkv, L0_attn_w_out, L0_attn_b_out, L0_ffn_gate_weight, L0_ffn_wi,
           L0_ffn_wo, L0_c, L0_wmod):
    import numpy as np
    import concourse.bacc as bacc
    from concourse.bass_utils import run_bass_kernel_spmd

    w_qkv, b_qkv = np.asarray(L0_attn_w_qkv), np.asarray(L0_attn_b_qkv)
    q, k = (w_qkv[i * D:(i + 1) * D].reshape(NG, HG * HD, D) for i in range(2))
    bq, bk = (b_qkv[i * D:(i + 1) * D].reshape(NG, HG * HD) for i in range(2))
    arrays = {
        "x": np.asarray(L0_attn_x)[0],
        "w_qk": np.concatenate([q, k], axis=1).reshape(NG * P, D).T,
        "b_qk": np.concatenate([bq, bk], axis=1).T,
        "w_v": w_qkv[2 * D:].T,
        "w_o": np.asarray(L0_attn_w_out).T,
        "b_rows": np.stack([b_qkv[2 * D:], np.asarray(L0_attn_b_out)]),
        "w_gate": np.asarray(L0_ffn_gate_weight).T,
        "w_in": np.asarray(L0_ffn_wi),
        "w_down": np.asarray(L0_ffn_wo),
        "c_col": np.asarray(L0_c)[0].reshape(DT, P).T,
        "w_mod": np.asarray(L0_wmod),
    }
    arrays = {n: np.ascontiguousarray(a) for n, a in arrays.items()}
    nc = bacc.Bacc("TRN2", target_bir_lowering=False, num_devices=1)
    args = {n: nc.dram_tensor(n, a.shape, mybir.dt.from_np(a.dtype), kind="ExternalInput").ap()
            for n, a in arrays.items()}
    result = nc.dram_tensor("out", (S, D), F32, kind="ExternalOutput").ap()
    layer(nc, *args.values(), result)
    r = run_bass_kernel_spmd(nc, [arrays], core_ids=[0])
    return r.results[0]["out"].reshape(1, S, D)
```

```python
from contextlib import ExitStack

import concourse.bass as bass
from concourse import mybir

F32 = mybir.dt.float32
BF16 = mybir.dt.bfloat16
F32R = mybir.dt.float32r
U32 = mybir.dt.uint32
I32 = mybir.dt.int32
ALU = mybir.AluOpType
ACT = mybir.ActivationFunctionType
AX = mybir.AxisListType

P = 128
D = 256
DT = D // P
S = 2048
NT = S // P
QB = 512
TB = QB // P
NB = S // QB
H = 16
HD = D // H
HG = 4
NG = H // HG
CT = 32
PARTS_Q = [0, 0, 1, 0, 1, 2]
PARTS_K = [0, 1, 0, 2, 1, 0]
KR = HD * len(PARTS_Q)
MR = 2 * HG
SCALE = HD ** -0.5
NEG = -3.0e38
E = 8
I = 1024
IT = I // P
CAP = 320
NS = E * CAP
ROW = 2 * D + 2
CT3 = -(-CAP // P)
CAPW = CT3 * P
LAST_ROWS = CAP - (CT3 - 1) * P
BIAS_FROM = (NG - 2) * NB
DOWN_LAG = 2
TAIL_TILES = (NB - 1) * TB
RSQRT_SEED = float(0x5F3759DF)
EPS = 1e-5


def block_units():
    return [[(qt, h, c) for qt in range(TB) for h in range(HG) for c in range(b + 1)] for b in range(NB)]


TENSOR_RATE, VECTOR_RATE, SCALAR_RATE = 2.4, 0.96, 1.2
VECTOR_FIXED, SCALAR_FIXED, MASK_TIME = 75, 60, 700
EARLY_BLOCKS, EARLY_SLOWER = 4, 1.0
SPLIT_LAG = 2500
SPLIT_TIME, STACK_TIME = 6000, 20000
PROJECT_FROM = {1: 0, 2: 1, 3: 6}
MAX_AHEAD = 0


def key_tiles(b):
    diag, full = [b * TB + j for j in range(TB)], list(range(b * TB))
    order = []
    for j in range(TB):
        order += [diag[j]] + full[j:j + 1]
    return order + full[TB:]


TAIL_LAG = TB + 2


def tail_slot(k, t0, t1):
    stages = (("turn", k), ("out", k - 1), ("turn_normal", k - TAIL_LAG), ("gate", k - TAIL_LAG - 1))
    return [ev for ev in stages if t0 <= ev[1] < t1]


def attention_plan():
    units = block_units()
    maxima = [(g, b, u) for g in range(NG) for b in range(NB) for u in range(len(units[b]))]
    plan = []
    now = 0.0
    vector = []
    scalar = []
    block = 0
    projections = [(g, b) for g in range(1, NG) for b in range(NB)]
    projected = -1e9
    split = None
    parts_at = {}
    scored_at = {-1: 0.0}
    waiting_rows = []

    def tensor(ns, after=0.0):
        nonlocal now
        now = max(now, after) + ns * (EARLY_SLOWER if block < EARLY_BLOCKS else 1.0)

    def bank_free(read):
        return read[-3] if len(read) >= 3 else 0.0

    def read_by(read, rate, fixed, width, latency=60):
        read.append(max(read[-1] if read else 0.0, now + latency) + width / rate + fixed)

    def emit_max():
        g, b, u = maxima[len(vector)]
        qt, h, c = units[b][u]
        width = QB if c < b else P * (qt + 1)
        plan.append(("max", len(vector), g, b, qt, h, c, width))
        tensor(width / TENSOR_RATE + 3, bank_free(vector))
        read_by(vector, VECTOR_RATE, VECTOR_FIXED, width)
        if u == len(units[b]) - 1:
            n = g * NB + b
            turn_rows(all_of=n - 2)
            plan.append(("max_parts", n))
            vector[-1] += 400
            waiting_rows.append([n, vector[-1] + 100])

    def turn_rows(all_of=-1):
        while waiting_rows and (waiting_rows[0][1] <= now or waiting_rows[0][0] <= all_of):
            n, formed = waiting_rows.pop(0)
            plan.append(("max_rows", n))
            tensor(300, formed)
            vector[-1] = max(vector[-1], now + 550) + 450

    def may_run():
        if len(vector) == len(maxima):
            return False
        g, b, u = maxima[len(vector)]
        if g <= block // NB:
            return True
        return (block % NB >= MAX_AHEAD and g in parts_at and g - 2 in scored_at
                and now >= max(parts_at[g], scored_at[g - 2]) + STACK_TIME)

    def fill(until=0.0):
        while may_run() and bank_free(vector) <= max(now, until):
            emit_max()
        turn_rows()

    def project():
        nonlocal split, projected
        if split and now >= projected + SPLIT_LAG:
            plan.append(("split", *split))
            split = None
        if projections and not split and block >= PROJECT_FROM[projections[0][0]] and now >= projected + SPLIT_TIME:
            split = projections.pop(0)
            plan.append(("project", *split))
            tensor(1800)
            projected = now
            if split[1] == NB - 1:
                parts_at[split[0]] = now + SPLIT_TIME

    weigh = None
    beside = [ev for k in range(TAIL_TILES + TAIL_LAG + 1) for ev in tail_slot(k, 0, TAIL_TILES)]
    beside.append(("rank", 0, TAIL_TILES))
    plan += [("normal", 0), ("normal", 1), ("prepare", 0), ("normal", 2), ("prepare", 1)]
    while maxima[len(vector)][:2] == (0, 0):
        emit_max()
    plan += [("normal", 3), ("prepare", 2), ("prepare", 3)]
    now += 12000
    for n in range(NG * NB):
        g, b = divmod(n, NB)
        block = n
        if b == 0:
            scored_at[g - 1] = now
        while len(vector) < len(maxima) and maxima[len(vector)][0] * NB + maxima[len(vector)][1] <= n:
            emit_max()
            turn_rows()
            project()
        turn_rows(all_of=n)
        for i, kt in enumerate(key_tiles(b)):
            width = QB - P * max(0, kt - b * TB)
            for h in range(HG):
                fill(bank_free(scalar))
                plan.append(("scores", n, kt, h))
                tensor(width / TENSOR_RATE + 3, bank_free(scalar))
                read_by(scalar, SCALAR_RATE, SCALAR_FIXED, width)
                if n == NG * NB - 1 and beside and i >= 1:
                    plan.append(beside.pop(0))
                    tensor(450)
                if h == 1 and n >= 1 and i == 1:
                    plan.append(("turn_heads", n - 1))
                    tensor(500)
                    if vector:
                        vector[-1] = max(vector[-1], now + 60) + 550
            if weigh is not None:
                fill(weigh[3])
                plan.append(("weigh", weigh[0], weigh[1]))
                tensor(HG * weigh[2] * 234 / QB, weigh[3])
                if weigh[0] < n:
                    plan.append(("heads_out", n - 1))
                    scalar[-1] = max(scalar[-1], now + 60) + 480
            weigh = (n, kt, width, scalar[-1] + 60 + (MASK_TIME if kt >= b * TB else 0))
            project()
    plan += beside
    plan.append(("gate_exp", 0, TAIL_TILES))
    plan.append(("weigh", weigh[0], weigh[1]))
    plan.append(("heads_out", weigh[0]))
    plan.append(("turn_heads", weigh[0]))
    for k in range(TAIL_TILES, NT + TAIL_LAG + 1):
        plan.extend(tail_slot(k, TAIL_TILES, NT))
    plan.append(("rank", TAIL_TILES, NT))
    plan.append(("gate_exp", TAIL_TILES, NT))
    return plan


def layer(nc, x, w_qk, b_qk, w_v, w_o, b_rows, w_gate, w_in, w_down, c_col, w_mod, out):
    qk_parts = nc.dram_tensor("qk_parts", (2, 3, P, S), BF16, kind="Internal").ap()
    slot_rows = nc.dram_tensor("slot_rows", (NS, ROW), F32, kind="Internal").ap()

    plan = attention_plan()
    misc_use = {}
    for ev in plan:
        if ev[0] == "prepare":
            misc_use["project", 0, ev[1]] = len(misc_use)
        if ev[0] in ("max_rows", "turn_heads", "project"):
            misc_use[ev] = len(misc_use)

    with ExitStack() as ctx:
        def sem(name):
            return ctx.enter_context(nc.semaphore(name))

        def sb(name, shape, dt):
            return ctx.enter_context(nc.sbuf_tensor(name, shape, dt))

        bank = [ctx.enter_context(nc.psum_tensor(f"bank{i}", [P, QB], F32)) for i in range(8)]
        MAX_BANKS, SCORE_BANKS, VALUE_BANK, MISC_BANK = (0, 1, 2), (3, 4, 5), 6, 7
        TURN_BANKS, V_BANKS = (3, 4), (5, 6)
        COUNT_BANK = 2
        DOWN_BANKS, SLOT_BANKS = (3, 4, 5), (6, 7)

        def tail_bank(stage, t):
            return stage + (3 if t >= TAIL_TILES and t % 2 else 0)

        token = sb("token", [P, NT, ROW], F32)
        x_sb = token[:, :, 0:D]
        heads = token[:, :, D:2 * D]
        prob = token[:, :, 2 * D]
        token_id = token[:, :, 2 * D + 1:ROW]
        w_o_sb = sb("w_o_sb", [P, DT, D], F32)
        w_gate_sb = sb("w_gate_sb", [P, DT, E], F32)
        gates = sb("gates", [P, 2, D], F32)
        mod_col = sb("mod_col", [P, 4, DT], F32)
        ident = sb("ident", [P, P], F32)
        stats = sb("stats", [P, NT, 6], F32)
        mean_var = sb("mean_var", [P, NT, 2], F32)
        root = sb("root", [P, 2, NT], F32)
        rstd = sb("rstd", [P, NT], F32)
        product = sb("product", [P, 2, D], F32)
        logits = sb("logits", [P, NT, E], F32)
        expd = sb("expd", [P, NT, E], F32)
        top = sb("top", [P, NT], F32)
        onehot = sb("onehot", [P, NT, E], F32)
        onehot_b = sb("onehot_b", [P, NT, E], BF16)
        order = sb("order", [P, NT, E], F32)
        first_slot = sb("first_slot", [P, NT, E], F32)
        earlier = sb("earlier", [P, NT + 1, E], F32)
        before = sb("before", [P, NT, E], F32)
        rank = sb("rank", [P, NT], F32)
        kept = sb("kept", [P, NT], F32)
        slot = sb("slot", [P, NT], F32)
        slot_to = sb("slot_to", [P, NT], U32)
        upper = sb("upper", [P, P], BF16)
        ones_b = sb("ones_b", [P, P], BF16)
        empty = sb("empty", [P, ROW], F32)
        attention = ExitStack()

        def sb1(name, shape, dt):
            return attention.enter_context(nc.sbuf_tensor(name, shape, dt))
        stacks = sb1("stacks", [P, 2, 2, HG, S], BF16)
        hT = sb1("hT", [P, DT, S], F32)
        v_sb = sb1("v_sb", [P, NT, H, CT], F32)
        probs = sb1("probs", [P, 3, HG, QB], F32)
        early = probs[:, :, :, :].rearrange("p a b c -> p (a b c)")
        w_mod_sb = early[:, 0:DT * 6 * D].rearrange("p (t n) -> p t n", t=DT)
        silu_rep = early[:, DT * 6 * D:DT * 6 * D + DT * P].rearrange("p (t n) -> p t n", t=DT)
        at = DT * 6 * D + DT * P
        xhat = early[:, at:at + 2 * TB * D].rearrange("p (t d) -> p t d", d=D)
        bias_row = early[0:1, at + 2 * TB * D:at + (2 * TB + 2) * D].rearrange("p (a d) -> p a d", a=2)
        bias_all = sb1("bias_all", [P, 2, D], F32)
        ident_b = sb1("ident_b", [P, P], BF16)
        ones_f = sb1("ones_f", [P, P], F32)
        w_qk_sb = sb1("w_qk_sb", [P, DT, NG * P], F32)
        w_v_sb = sb1("w_v_sb", [P, DT, D], F32)
        qk_sb = sb1("qk_sb", [P, QB], F32)
        rest = sb1("rest", [P, QB], F32)
        oT_sb = qk_sb[:, :].rearrange("p (r n) -> p r n", r=2)
        h2T = rest[:, :].rearrange("p (r n) -> p r n", r=2)
        part = sb1("part", [P, 3, QB], BF16)
        b_qk_sb = sb1("b_qk_sb", [P, NG], F32)
        qk_scale = sb1("qk_scale", [P, 1], F32)
        c_sb = sb1("c_sb", [P, DT], F32)
        c_tmp = sb1("c_tmp", [P, 3, DT], F32)
        silu = sb1("silu", [P, DT], F32)
        sign = product
        causal = sb1("causal", [P, QB], F32)
        masked = sb1("masked", [P, 3, QB], BF16)
        head_sel = sb1("head_sel", [P, HG], F32)
        chunk_max = sb1("chunk_max", [P, 2, TB * HG, NB], F32)
        neg_max = sb1("neg_max", [P, TB * HG], F32)
        max_part = sb1("max_part", [P, 2, TB * HG, 2], BF16)
        o_sb = sb1("o_sb", [P, 2, QB], F32)
        inv_sum = sb1("inv_sum", [P, TB * HG], F32)
        attention.close()
        WN = 2 * DT * I
        w_raw = sb("w_raw", [P, 2, WN], F32)
        w_split = [sb("w_split0", [P, 2, WN], F32R)]
        w_split.append(sb("w_split1", [P, 2, WN], F32R))
        SR = 3
        slots_sb = sb("slots_sb", [P, SR, CT3, ROW], F32)
        slotT = sb("slotT", [P, 2, 2, DT, CAP], F32R)
        slotT_raw = sb("slotT_raw", [P, DT, CAP], F32)
        act_raw = sb("act_raw", [P, 2, CAP], F32)
        AR = 3
        acts = sb("acts", [P, AR, 2, CAPW], F32R)
        down = sb("down", [P, 2, CT3, D], F32)

        loaded_c = sem("loaded_c")
        loaded_shift = sem("loaded_shift")
        loaded_mod = sem("loaded_mod")
        loaded_x = [sem(f"loaded_x{b}") for b in range(NB)]
        loaded_qkv = sem("loaded_qkv")
        loaded_late = sem("loaded_late")
        pool_consts = sem("pool_consts")
        pool_chain = sem("pool_chain")
        v_zeroed = sem("v_zeroed")
        c_exp = sem("c_exp")
        silu_ready = sem("silu_ready")
        mods_done = sem("mods_done")
        mods_read = sem("mods_read")
        dve_chain = sem("dve_chain")
        xhat_ready = sem("xhat_ready")
        xhat_turned = sem("xhat_turned")
        hT_ready = sem("hT_ready")
        v_done = sem("v_done")
        v_read = sem("v_read")
        x_biased = sem("x_biased")
        misc_done = sem("misc_done")
        misc_read_a = sem("misc_read_a")
        misc_read_v = sem("misc_read_v")
        part0_ready = sem("part0_ready")
        rest_ready_v = sem("rest_ready_v")
        rest_ready_p = sem("rest_ready_p")
        part1_ready = sem("part1_ready")
        qk_split_v = sem("qk_split_v")
        qk_split_p = sem("qk_split_p")
        parts_stored = sem("parts_stored")
        STACK_DMAS = 2 * len(PARTS_Q)
        stacked = [sem(f"stacked{g}") for g in range(NG)]
        stacked_first = [sem(f"stacked_first{b}") for b in range(NB)]
        ones_rows = sem("ones_rows")
        max_scored = sem("max_scored")
        max_read = sem("max_read")
        max_parts = sem("max_parts")
        max_row0 = sem("max_row0")
        max_rows = sem("max_rows")
        scored = sem("scored")
        exp_done = sem("exp_done")
        diag_done = sem("diag_done")
        weighted = sem("weighted")
        o_read = sem("o_read")
        heads_ready = sem("heads_ready")
        empty_ready = sem("empty_ready")
        causal_ready = sem("causal_ready")
        pads_zeroed = sem("pads_zeroed")
        slots_emptied = sem("slots_emptied")
        heads_turned = sem("heads_turned")
        oT_ready = sem("oT_ready")
        projected = sem("projected")
        x1_ready = sem("x1_ready")
        xhat2_ready = sem("xhat2_ready")
        xhat2_turned = sem("xhat2_turned")
        h2T_ready = sem("h2T_ready")
        gated = sem("gated")
        exp_gate = sem("exp_gate")
        top_ready = sem("top_ready")
        logits_read = sem("logits_read")
        onehot_ready = sem("onehot_ready")
        counted = sem("counted")
        counts_read = sem("counts_read")
        slots_known = sem("slots_known")
        scattered = sem("scattered")
        slots_loaded = [sem(f"slots_loaded{r}") for r in range(SR)]
        slots_turned = sem("slots_turned")
        slotT_high = sem("slotT_high")
        slotT_raw_done = sem("slotT_raw_done")
        slotT_ready = sem("slotT_ready")
        w_loaded = [sem(f"w_loaded{r}") for r in range(2)]
        w_high = sem("w_high")
        w_ready = sem("w_ready")
        up_done = sem("up_done")
        gelu_done = sem("gelu_done")
        act_ready = sem("act_ready")
        act_used = sem("act_used")
        down_done = sem("down_done")
        down_read = sem("down_read")
        rows_ready = sem("rows_ready")
        kept_stored = sem("kept_stored")
        rows_stored = [sem(f"rows_stored{r}") for r in range(2)]

        step_of = {}
        for n in range(NG * NB):
            for kt in key_tiles(n % NB):
                step_of[n, kt] = len(step_of)
        last_step = [step_of[n, key_tiles(n % NB)[-1]] for n in range(NG * NB)]
        units_before = [0]
        for g in range(NG):
            for u in block_units():
                units_before.append(units_before[-1] + len(u))

        def misc_reads(index):
            kinds = [k[0] for k, i in misc_use.items() if i < index]
            return sum(k != "turn_heads" for k in kinds), sum(k == "turn_heads" for k in kinds)

        def stack(g, side):
            return stacks[:, g % 2, side, :, :]

        CH = 4
        CW = WN // CH

        def chunk(w, c):
            return w[:, c * CW:(c + 1) * CW]

        block = ctx.enter_context(nc.Block())

        def load_expert(eng, e):
            w = w_raw[:, e % 2, :]
            eng.dma_start(w[:, 0:DT * I].rearrange("p (t n) -> p t n", t=DT),
                          w_in[e].rearrange("(t p) n -> p t n", p=P)).then_inc(w_loaded[e % 2], 16)
            eng.dma_start(w[:, DT * I:].rearrange("p (t n) -> p t n", t=IT),
                          w_down[e].rearrange("(t p) n -> p t n", p=P)).then_inc(w_loaded[e % 2], 16)

        def load_slots(eng, e):
            rows = slot_rows[e * CAP:(e + 1) * CAP, :]
            eng.dma_start(slots_sb[:, e % SR, 0:CT3 - 1, :],
                          rows[0:(CT3 - 1) * P, :].rearrange("(t p) d -> p t d", p=P)).then_inc(slots_loaded[e % SR], 16)
            eng.dma_start(slots_sb[0:LAST_ROWS, e % SR, CT3 - 1, :],
                          rows[(CT3 - 1) * P:CAP, :]).then_inc(slots_loaded[e % SR], 16)

        def rows_of(st):
            return min(P, CAP - st * P)

        @block.sync
        def _(sp):
            sp.dma_start(c_sb[:, :], c_col).then_inc(loaded_c, 16)
            sp.dma_start(x_sb[:, 0:TB, :], x[0:QB, :].rearrange("(t p) d -> p t d", p=P)).then_inc(loaded_x[0], 16)
            sp.dma_start(w_mod_sb[:, :, 0:2 * D], w_mod[:, 0:2 * D].rearrange("(t p) n -> p t n", p=P))\
              .then_inc(loaded_shift, 16)
            sp.dma_start(bias_row, b_rows.rearrange("(a t) d -> a t d", a=1)).then_inc(loaded_shift, 16)
            sp.dma_start(w_qk_sb[:, :, :], w_qk.rearrange("(t p) n -> p t n", p=P)).then_inc(loaded_qkv, 16)
            sp.dma_start(b_qk_sb[:, :], b_qk).then_inc(loaded_qkv, 16)
            sp.dma_start(w_v_sb[:, :, :], w_v.rearrange("(t p) n -> p t n", p=P)).then_inc(loaded_qkv, 16)
            for b in range(1, NB):
                sp.dma_start(x_sb[:, b * TB:(b + 1) * TB, :],
                             x[b * QB:(b + 1) * QB, :].rearrange("(t p) d -> p t d", p=P)).then_inc(loaded_x[b], 16)
                if b == 1:
                    sp.dma_start(w_mod_sb[:, :, 2 * D:], w_mod[:, 2 * D:].rearrange("(t p) n -> p t n", p=P))\
                      .then_inc(loaded_mod, 16)
            sp.dma_start(w_o_sb[:, :, :], w_o.rearrange("(t p) n -> p t n", p=P)).then_inc(loaded_late, 16)
            sp.dma_start(w_gate_sb[:, :, :], w_gate.rearrange("(t p) n -> p t n", p=P)).then_inc(loaded_late, 16)
            for b in range(NB):
                cols = slice(b * QB, (b + 1) * QB)
                sp.wait_ge(qk_split_v, b + 1)
                sp.dma_start(qk_parts[0, :, :, cols].rearrange("a p s -> p a s"), part[:, :, :]).then_inc(parts_stored, 16)
                sp.wait_ge(parts_stored, 16 * (b + 1))
                for r in range(len(PARTS_Q)):
                    for side, parts in ((0, PARTS_Q), (1, PARTS_K)):
                        sp.dma_start(stack(0, side)[HD * r:HD * (r + 1), :, cols],
                                     qk_parts[0, parts[r], side * P // 2:(side + 1) * P // 2, cols]
                                     .rearrange("(h i) s -> i h s", i=HD)).then_inc(stacked_first[b], 16)
            for b in range(NB):
                sp.wait_ge(stacked_first[b], STACK_DMAS * 16)
            for g in range(1, NG):
                if g >= 3:
                    sp.wait_ge(stacked[g - 2], 16 * STACK_DMAS)
                for b in range(NB):
                    sp.wait_ge(qk_split_p, (g - 1) * NB + b + 1)
                    sp.dma_start(qk_parts[g % 2, :, :, b * QB:(b + 1) * QB].rearrange("a p s -> p a s"),
                                 part[:, :, :]).then_inc(parts_stored, 16)
                sp.wait_ge(parts_stored, 16 * NB * (g + 1))
                if g >= 2:
                    sp.wait_ge(scored, HG * (last_step[(g - 1) * NB - 1] + 1))
                for r in range(len(PARTS_Q)):
                    for side, parts in ((0, PARTS_Q), (1, PARTS_K)):
                        sp.dma_start(stack(g, side)[HD * r:HD * (r + 1)],
                                     qk_parts[g % 2, parts[r], side * P // 2:(side + 1) * P // 2, :]
                                     .rearrange("(h i) s -> i h s", i=HD)).then_inc(stacked[g], 16)
            sp.wait_ge(empty_ready, 1)
            sp.dma_start(slot_rows.rearrange("(t p) d -> p t d", p=P),
                         empty[:, :].rearrange("p (t d) -> p t d", t=1).broadcast_to([P, NS // P, ROW]))\
              .then_inc(slots_emptied, 16)
            even = (NG - 1) * NB
            sp.wait_ge(scored, HG * (last_step[even - 1] + 1))
            sp.wait_ge(max_scored, units_before[even])
            for e in range(2):
                load_expert(sp, e)
            for b in range(NB):
                sp.wait_ge(x1_ready, (b + 1) * TB)
                sp.dma_start(out[b * QB:(b + 1) * QB, :].rearrange("(t p) d -> p t d", p=P),
                             x_sb[:, b * TB:(b + 1) * TB, :]).then_inc(kept_stored, 16)
            sp.wait_ge(scattered, 16 * NT)
            for e in range(SR):
                load_slots(sp, e)
            for e in range(E):
                if e >= 2:
                    sp.wait_ge(w_ready, CH * (e - 1))
                    load_expert(sp, e)
                if e >= SR:
                    f = e - SR
                    sp.wait_ge(rows_stored[f % 2], 16 * CT3 * (f // 2 + 1))
                    load_slots(sp, e)

        def leave_part0(eng, n, done):
            eng.wait_ge(part0_ready, n + 1)
            eng.tensor_tensor(rest[:, :], qk_sb[:, :], part[:, 0, :], ALU.subtract).then_inc(done, 1)

        def leave_part1(eng, n, done):
            eng.wait_ge(part1_ready, n + 1)
            eng.tensor_tensor(part[:, 2, :], rest[:, :], part[:, 1, :], ALU.subtract).then_inc(done, 1)

        @block.gpsimd
        def _(pool):
            chain = [0]

            def link(ins):
                chain[0] += 1
                ins.then_inc(pool_chain, 1)
                pool.wait_ge(pool_chain, chain[0])

            link(pool.memset(ones_f[:, :], 1.0))
            link(pool.memset(ones_b[:, :], 1.0))
            link(pool.memset(qk_scale[0:P // 2, :], SCALE))
            link(pool.memset(qk_scale[P // 2:P, :], 1.0))
            link(pool.memset(head_sel[:, :], 1.0))
            rows = head_sel[KR:KR + MR, :]
            link(pool.affine_select(out=rows, in_=rows, compare_op=ALU.is_ge, fill=0.0, base=0,
                                    pattern=[[-2, HG]], channel_multiplier=1))
            link(pool.affine_select(out=rows, in_=rows, compare_op=ALU.is_ge, fill=0.0, base=1,
                                    pattern=[[2, HG]], channel_multiplier=-1))
            link(pool.memset(ident[:, :], 0.0))
            link(pool.affine_select(out=ident[:, :], in_=ident[:, :], compare_op=ALU.not_equal, fill=1.0, base=0,
                                    pattern=[[-1, P]], channel_multiplier=1))
            link(pool.tensor_copy(ident_b[:, :], ident[:, :]))
            pool.memset(ones_f[0:1, 0:1], 1.0).then_inc(pool_consts, 1)
            link(pool.memset(v_sb[:, :, :, :], 0.0))
            pool.memset(v_sb[:, :, :, HD:HD + 1], 1.0).then_inc(v_zeroed, 1)
            link(pool.memset(causal[:, :], 0.0))
            pool.affine_select(out=causal[:, QB - P:QB], in_=causal[:, QB - P:QB], compare_op=ALU.is_ge,
                               fill=NEG, base=0, pattern=[[-1, P]], channel_multiplier=1).then_inc(causal_ready, 1)
            link(pool.affine_select(out=upper[:, :], in_=ones_b[:, :], compare_op=ALU.is_gt, fill=0.0, base=0,
                                    pattern=[[1, P]], channel_multiplier=-1))
            for e in range(E):
                pool.memset(order[:, :, e], float(E - e))
                last = pool.memset(first_slot[:, :, e], float(CAP * e))
            link(last)
            link(pool.memset(earlier[:, 0, :], 0.0))
            link(pool.iota(token_id.bitcast(I32), pattern=[[P, NT]], base=0, channel_multiplier=1))
            link(pool.memset(empty[:, :], 0.0))
            pool.memset(empty[:, ROW - 1:ROW].bitcast(I32), S).then_inc(empty_ready, 1)

            biased = 0
            for ev in plan:
                if ev[0] == "project":
                    leave_part0(pool, ev[1] * NB + ev[2], rest_ready_p)
                if ev[0] == "split":
                    leave_part1(pool, ev[1] * NB + ev[2], qk_split_p)
                if ev[0] == "scores" and ev[3] == HG - 1:
                    _, n, kt, h = ev
                    j = kt - (n % NB) * TB
                    if j >= 0:
                        s = step_of[n, kt]
                        pool.wait_ge(exp_done, HG * (s + 1))
                        d = probs[:, s % 3, :, 0:P]
                        pool.affine_select(out=d, in_=d, compare_op=ALU.is_ge, fill=0.0, base=0,
                                           pattern=[[0, HG], [1, P]], channel_multiplier=-1).then_inc(diag_done, 1)
                    if j >= 0 and BIAS_FROM <= n and biased < NT:
                        if biased == 0:
                            pool.wait_ge(mods_read, 4)
                            pool.wait_ge(xhat_ready, NT)
                            link(pool.tensor_tensor(product[:, 0, :], gates[:, 0, :], bias_all[:, 1, :], ALU.mult))
                        pool.tensor_tensor(x_sb[:, biased, :], x_sb[:, biased, :], product[:, 0, :], ALU.add)\
                            .then_inc(x_biased, 1)
                        biased += 1
                if ev[0] == "rank":
                    _, t0, t1 = ev
                    if t0 == 0:
                        pool.wait_ge(slots_emptied, 16)
                    pool.wait_ge(slots_known, 1 if t0 == 0 else 2)
                    for t in range(t0, t1):
                        pool.indirect_dma_start(
                            out=slot_rows, out_offset=bass.IndirectOffsetOnAxis(ap=slot_to[:, t:t + 1], axis=0),
                            in_=token[:, t, :], in_offset=None, bounds_check=NS - 1, oob_is_err=False)\
                            .then_inc(scattered, 16)
            pool.wait_ge(kept_stored, 16 * NB)
            for e in range(E):
                for st in range(CT3):
                    rows = rows_of(st)
                    pool.wait_ge(rows_ready, CT3 * e + st + 1)
                    pool.indirect_dma_start(
                        out=out, out_offset=bass.IndirectOffsetOnAxis(
                            ap=slots_sb[0:rows, e % SR, st, ROW - 1:ROW].bitcast(U32), axis=0),
                        in_=down[0:rows, e % 2, st, :], in_offset=None, bounds_check=S - 1, oob_is_err=False)\
                        .then_inc(rows_stored[e % 2], 16)
            for r in range(2):
                pool.wait_ge(rows_stored[r], 16 * CT3 * E // 2)

        @block.scalar
        def _(act):
            act.wait_ge(loaded_c, 16)
            act.activation(c_tmp[:, 0, :], c_sb[:, :], ACT.Exp, scale=-1.0).then_inc(c_exp, 1)

            def make_ones_row(par, h):
                row = act.activation(stacks[KR:KR + MR, par, 1, h, :], ones_b[KR:KR + MR, 0:1].broadcast_to([MR, S]),
                                     ACT.Copy, scale=head_sel[KR:KR + MR, h:h + 1])
                if h == HG - 1:
                    row.then_inc(ones_rows, 1)
            act.wait_ge(pool_consts, 1)
            for h in range(HG):
                make_ones_row(0, h)

            def read_projection(g, b):
                n = g * NB + b
                act.wait_ge(misc_done, misc_use["project", g, b] + 1)
                if n >= 1:
                    act.wait_ge(rest_ready_v if n <= NB else rest_ready_p, n if n <= NB else n - NB)
                act.activation(qk_sb[:, :], bank[MISC_BANK][:, :], ACT.Identity, bias=b_qk_sb[:, g:g + 1],
                               scale=qk_scale[:, 0:1]).then_inc(misc_read_a, 1)
                act.wait_ge(misc_read_a, misc_reads(misc_use["project", g, b])[0] + 1)
                if n >= 1:
                    act.wait_ge(parts_stored, 16 * n)
                act.copy(part[:, 0, :], qk_sb[:, :]).then_inc(part0_ready, 1)

            def second_part(g, b):
                n = g * NB + b
                act.wait_ge(rest_ready_v if g == 0 else rest_ready_p, n + 1 if g == 0 else n + 1 - NB)
                act.copy(part[:, 1, :], rest[:, :]).then_inc(part1_ready, 1)

            for ev in plan:
                if ev[0] == "prepare":
                    b = ev[1]
                    if b == 0:
                        act.wait_ge(mods_read, 1)
                    for ft in range(DT):
                        act.wait_ge(xhat_turned, b * DT + ft + 1)
                        act.activation(hT[:, ft, b * QB:(b + 1) * QB], bank[TURN_BANKS[ft]][:, :], ACT.Identity,
                                       bias=mod_col[:, 0, ft:ft + 1], scale=mod_col[:, 1, ft:ft + 1]).then_inc(hT_ready, 1)
                    if b == 0:
                        act.wait_ge(silu_ready, 2)
                    read_projection(0, b)
                    second_part(0, b)
                if ev[0] == "project":
                    read_projection(ev[1], ev[2])
                    if ev[1] == 1:
                        make_ones_row(1, ev[2])
                if ev[0] == "split":
                    second_part(ev[1], ev[2])
                if ev[0] == "max_rows":
                    n = ev[1]
                    g, b = divmod(n, NB)
                    act.wait_ge(misc_done, misc_use[ev] + 1)
                    act.copy(stack(g, 0)[KR:KR + MR, 0, b * QB:(b + 1) * QB],
                             bank[MISC_BANK][:, :].bitcast(BF16)[0:MR, 0:QB]).then_inc(misc_read_a, 1)
                    act.wait_ge(misc_read_a, misc_reads(misc_use[ev])[0] + 1)
                    act.copy(c_tmp[0:1, 1, 0:1], c_tmp[0:1, 0, 0:1]).then_inc(max_row0, 1)
                if ev[0] == "scores":
                    _, n, kt, h = ev
                    s = step_of[n, kt]
                    u = HG * s + h
                    width = QB - P * max(0, kt - (n % NB) * TB)
                    act.wait_ge(scored, u + 1)
                    if h == 0 and s >= 3:
                        act.wait_ge(weighted, s - 2)
                    act.activation(probs[:, s % 3, h, 0:width], bank[SCORE_BANKS[u % 3]][:, 0:width], ACT.Exp)\
                        .then_inc(exp_done, 1)
                if ev[0] == "heads_out":
                    n = ev[1]
                    act.wait_ge(weighted, last_step[n] + 1)
                    if n >= 2:
                        act.wait_ge(misc_done, misc_use["turn_heads", n - 2] + 1)
                    act.copy(o_sb[:, n % 2, :], bank[VALUE_BANK][:, :]).then_inc(o_read, 1)
                if ev[0] == "turn":
                    t = ev[1]
                    act.wait_ge(heads_turned, t + 1)
                    if t >= 2:
                        act.wait_ge(projected, t - 1)
                    act.copy(oT_sb[:, t % 2, :], bank[tail_bank(0, t)][:, 0:D]).then_inc(oT_ready, 1)
                if ev[0] == "turn_normal":
                    t = ev[1]
                    act.wait_ge(xhat2_turned, t + 1)
                    if t >= 2:
                        act.wait_ge(gated, t - 1)
                    for ft in range(DT):
                        act.activation(h2T[:, t % 2, ft * P:(ft + 1) * P], bank[tail_bank(2, t)][:, ft * P:(ft + 1) * P],
                                       ACT.Identity, bias=mod_col[:, 2, ft:ft + 1],
                                       scale=mod_col[:, 3, ft:ft + 1]).then_inc(h2T_ready, 1)
                if ev[0] == "gate_exp":
                    _, t0, t1 = ev
                    act.wait_ge(top_ready, 1 if t0 == 0 else 2)
                    act.activation(expd[:, t0:t1, :], expd[:, t0:t1, :], ACT.Exp).then_inc(exp_gate, 1)

            def split_weights(e, c):
                if c == 0:
                    act.wait_ge(w_loaded[e % 2], 32 * (e // 2 + 1))
                if e >= 2 and c == 0:
                    act.wait_ge(down_done, CT3 * (e - 1))
                act.copy(chunk(w_split[e % 2][:, 0, :], c), chunk(w_raw[:, e % 2, :], c)).then_inc(w_high, 1)

            def split_slots(e):
                for ft in range(DT):
                    act.wait_ge(slots_turned, e * DT + ft + 1)
                    act.activation(slotT[:, e % 2, 0, ft, :], bank[SLOT_BANKS[ft]][:, 0:CAP], ACT.Identity,
                                   bias=mod_col[:, 2, ft:ft + 1], scale=mod_col[:, 3, ft:ft + 1]).then_inc(slotT_high, 1)

            act.activation(c_tmp[0:1, 2, 0:1], c_tmp[0:1, 0, 0:1], ACT.Gelu)
            act.wait_ge(max_scored, units_before[-1])
            for c in range(CH):
                split_weights(0, c)
            split_slots(0)
            for n in range(E * IT):
                e, it = divmod(n, IT)
                act.wait_ge(up_done, n + 1)
                if n >= AR:
                    m = n - AR
                    act.wait_ge(act_used, (IT - 1) * (m // IT) + min(m % IT + 1, IT - 1))
                    if m % IT == IT - 1:
                        act.wait_ge(down_done, CT3 * (m // IT + 1))
                act.activation(acts[:, n % AR, 0, 0:CAP], bank[n % 3][:, 0:CAP], ACT.Gelu)
                if n >= 2:
                    act.wait_ge(act_ready, n - 1)
                act.activation(act_raw[:, n % 2, :], bank[n % 3][:, 0:CAP], ACT.Gelu).then_inc(gelu_done, 1)
                if e + 1 < E and 2 <= it < 2 + CH:
                    split_weights(e + 1, it - 2)
                if e + 1 < E and it == 6:
                    split_slots(e + 1)

        @block.vector
        def _(dve):
            chain = [0]

            def link(ins):
                chain[0] += 1
                ins.then_inc(dve_chain, 1)
                dve.wait_ge(dve_chain, chain[0])

            dve.wait_ge(c_exp, 1)
            link(dve.tensor_scalar(c_tmp[:, 1, :], c_tmp[:, 0, :], 1.0, None, ALU.add))
            link(dve.reciprocal(c_tmp[:, 2, :], c_tmp[:, 1, :]))
            dve.tensor_tensor(silu[:, :], c_sb[:, :], c_tmp[:, 2, :], ALU.mult).then_inc(silu_ready, 1)

            def inverse_root(b):
                ts = slice(b * TB, (b + 1) * TB)
                v, y, y_next = root[:, 0, ts], rstd[:, ts], root[:, 1, ts]
                link(dve.tensor_scalar(v, mean_var[:, ts, 1], EPS, None, ALU.add))
                link(dve.tensor_scalar(y_next.bitcast(I32), v.bitcast(I32), 1, None, ALU.logical_shift_right))
                link(dve.tensor_scalar(y.bitcast(I32), y_next.bitcast(I32), -1.0, RSQRT_SEED, ALU.mult, ALU.add))
                for _ in range(3):
                    link(dve.tensor_tensor(y_next, y, y, ALU.mult))
                    link(dve.tensor_tensor(y_next, y_next, v, ALU.mult))
                    link(dve.tensor_scalar(y_next, y_next, -0.5, 1.5, ALU.mult, ALU.add))
                    link(dve.tensor_tensor(y, y, y_next, ALU.mult))

            def normal(b):
                tiles = range(b * TB, (b + 1) * TB)
                dve.wait_ge(loaded_x[b], 16)
                for t in tiles:
                    last = dve.bn_stats(stats[:, t, :], x_sb[:, t, :])
                link(last)
                for t in tiles:
                    last = dve.bn_aggr(mean_var[:, t, :], stats[:, t, :])
                link(last)
                inverse_root(b)
                if b >= 2:
                    dve.wait_ge(xhat_turned, (b - 1) * DT)
                for t in tiles:
                    dve.tensor_scalar(xhat[:, t % (2 * TB), :], x_sb[:, t, :], mean_var[:, t, 0:1], rstd[:, t:t + 1],
                                      ALU.subtract, ALU.mult).then_inc(xhat_ready, 1)

            def read_mods(first):
                dve.wait_ge(mods_done, 1 if first else 2)
                mods = bank[2][:, 0:4 * DT].rearrange("p (m t) -> p m t", m=4)
                for m in ((0, 1) if first else (2, 3)):
                    last = dve.tensor_scalar(mod_col[:, m, :], mods[:, m, :], float(m % 2), None, ALU.add)
                last.then_inc(mods_read, 1)
                if first:
                    dve.tensor_copy(bias_all[:, :, :].rearrange("p a d -> p (a d)"), bank[1][:, :]).then_inc(mods_read, 1)
                else:
                    g2 = gates[:, :, :].rearrange("p a d -> p (a d)")
                    s2 = sign[:, :, :].rearrange("p a d -> p (a d)")
                    link(dve.tensor_scalar(s2, bank[0][:, :], 0.0, 2.0, ALU.is_ge, ALU.mult))
                    link(dve.tensor_scalar(s2, s2, -1.0, None, ALU.add))
                    link(dve.tensor_tensor(g2, bank[0][:, :], s2, ALU.mult))
                    link(dve.tensor_scalar(g2, g2, 0.25, None, ALU.max))
                    dve.tensor_tensor(g2, g2, s2, ALU.mult).then_inc(mods_read, 1)

            def prepare(b):
                if b == 0:
                    dve.wait_ge(v_zeroed, 1)
                    dve.wait_ge(mods_read, 2)
                leave_part0(dve, b, rest_ready_v)
                for t in range(b * TB, (b + 1) * TB):
                    dve.wait_ge(v_done, t + 1)
                    dve.tensor_tensor(v_sb[:, t, :, 0:HD],
                                      bank[V_BANKS[t % 2]][:, 0:D].rearrange("p (h i) -> p h i", h=H),
                                      bias_all[:, 0, :].rearrange("p (h i) -> p h i", h=H), ALU.add).then_inc(v_read, 1)
                leave_part1(dve, b, qk_split_v)

            def after_projection(t):
                if t == 0:
                    dve.wait_ge(x_biased, NT)
                dve.wait_ge(projected, t + 1)
                link(dve.tensor_tensor(product[:, t % 2, :], bank[tail_bank(1, t)][:, 0:D], gates[:, 0, :], ALU.mult))
                dve.tensor_tensor(x_sb[:, t, :], x_sb[:, t, :], product[:, t % 2, :], ALU.add).then_inc(x1_ready, 1)
                dve.wait_ge(x1_ready, t + 1)
                link(dve.bn_stats(stats[:, t, :], x_sb[:, t, :]))
                link(dve.bn_aggr(mean_var[:, t, :], stats[:, t, :]))
                if t % TB == TB - 1:
                    inverse_root(t // TB)
                    for i in range(t + 1 - TB, t + 1):
                        dve.tensor_scalar(heads[:, i, :], x_sb[:, i, :], mean_var[:, i, 0:1], rstd[:, i:i + 1],
                                          ALU.subtract, ALU.mult).then_inc(xhat2_ready, 1)

            def choose(part_no, t0, t1):
                ts = slice(t0, t1)
                n = t1 - t0

                def wide(a):
                    return a.rearrange("p (t e) -> p t e", e=1).broadcast_to([P, n, E])

                def counts(i):
                    return bank[COUNT_BANK][:, i * NT * E:i * NT * E + n * E].rearrange("p (t e) -> p t e", e=E)
                dve.wait_ge(gated, t1)
                dve.tensor_copy(logits[:, ts, :], bank[MISC_BANK][:, t0 * E:t1 * E].rearrange("p (t e) -> p t e", e=E))\
                   .then_inc(logits_read, 1)
                dve.wait_ge(logits_read, part_no + 1)
                link(dve.tensor_reduce(top[:, ts], logits[:, ts, :], AX.X, ALU.max))
                dve.tensor_tensor(expd[:, ts, :], logits[:, ts, :], wide(top[:, ts]), ALU.subtract).then_inc(top_ready, 1)
                link(dve.tensor_tensor(onehot[:, ts, :], logits[:, ts, :], wide(top[:, ts]), ALU.is_ge))
                link(dve.tensor_tensor(onehot[:, ts, :], onehot[:, ts, :], order[:, ts, :], ALU.mult))
                link(dve.tensor_reduce(top[:, ts], onehot[:, ts, :], AX.X, ALU.max))
                link(dve.tensor_tensor(onehot[:, ts, :], onehot[:, ts, :], wide(top[:, ts]), ALU.is_equal))
                dve.tensor_copy(onehot_b[:, ts, :], onehot[:, ts, :]).then_inc(onehot_ready, 1)
                link(dve.tensor_tensor(logits[:, ts, :], onehot[:, ts, :], first_slot[:, ts, :], ALU.mult))
                link(dve.tensor_reduce(slot[:, ts], logits[:, ts, :], AX.X, ALU.add))
                dve.wait_ge(counted, part_no + 1)
                link(dve.tensor_copy(before[:, ts, :], counts(1)))
                for t in range(t0, t1):
                    link(dve.tensor_tensor(earlier[:, t + 1, :], earlier[:, t, :], before[:, t, :], ALU.add))
                dve.tensor_tensor(before[:, ts, :], counts(0), earlier[:, ts, :], ALU.add).then_inc(counts_read, 1)
                dve.wait_ge(counts_read, part_no + 1)
                link(dve.tensor_tensor(before[:, ts, :], before[:, ts, :], onehot[:, ts, :], ALU.mult))
                link(dve.tensor_reduce(rank[:, ts], before[:, ts, :], AX.X, ALU.add))
                link(dve.tensor_tensor(slot[:, ts], slot[:, ts], rank[:, ts], ALU.add))
                link(dve.tensor_scalar(kept[:, ts], rank[:, ts], float(CAP), float(NS), ALU.is_ge, ALU.mult))
                link(dve.tensor_tensor(slot[:, ts], slot[:, ts], kept[:, ts], ALU.add))
                link(dve.tensor_copy(slot_to[:, ts], slot[:, ts]))
                dve.wait_ge(exp_gate, part_no + 1)
                link(dve.tensor_reduce(top[:, ts], expd[:, ts, :], AX.X, ALU.add))
                dve.reciprocal(prob[:, ts], top[:, ts]).then_inc(slots_known, 1)

            for ev in plan:
                if ev[0] == "normal":
                    normal(ev[1])
                    if ev[1] == 0:
                        dve.wait_ge(pool_consts, 1)
                        dve.wait_ge(silu_ready, 1)
                        for ft in range(DT):
                            last = dve.tensor_scalar(silu_rep[:, ft, :], ones_f[:, :], silu[:, ft:ft + 1], None, ALU.mult)
                        dve.wait_ge(loaded_qkv, 48)
                        link(last)
                        dve.tensor_scalar(b_qk_sb[:, :], b_qk_sb[:, :], qk_scale[:, 0:1], None, ALU.mult)\
                           .then_inc(silu_ready, 1)
                        read_mods(True)
                if ev[0] == "prepare":
                    prepare(ev[1])
                    if ev[1] == 0:
                        read_mods(False)
                if ev[0] == "max":
                    _, u, g, b, qt, h, c, width = ev
                    n = g * NB + b
                    src = bank[MAX_BANKS[u % 3]]
                    to = chunk_max[:, n % 2, qt * HG + h, c:c + 1]
                    dve.wait_ge(max_scored, u + 1)
                    if c < b:
                        dve.tensor_reduce(to, src[:, 0:QB], AX.X, ALU.max).then_inc(max_read, 1)
                    else:
                        if u >= 3:
                            dve.wait_ge(max_read, u - 2)
                        if u == 0:
                            dve.wait_ge(causal_ready, 1)
                        dve.tensor_tensor_reduce(out=masked[:, u % 3, 0:width], in0=src[:, 0:width],
                                                 in1=causal[:, QB - width:QB], scale=1.0, scalar=NEG, op0=ALU.add,
                                                 op1=ALU.max, accum_out=to).then_inc(max_read, 1)
                if ev[0] == "max_parts":
                    n = ev[1]
                    b = n % NB
                    dve.wait_ge(max_read, units_before[n + 1])
                    link(dve.tensor_reduce(neg_max[:, :], chunk_max[:, n % 2, :, 0:b + 1], AX.X, ALU.max, negate=True))
                    if n >= 2:
                        dve.wait_ge(misc_done, misc_use["max_rows", n - 2] + 1)
                    link(dve.tensor_copy(max_part[:, n % 2, :, 0], neg_max[:, :]))
                    dve.tensor_tensor(max_part[:, n % 2, :, 1], neg_max[:, :], max_part[:, n % 2, :, 0], ALU.subtract)\
                        .then_inc(max_parts, 1)
                if ev[0] == "max_rows":
                    n = ev[1]
                    g, b = divmod(n, NB)
                    rows = stack(g, 0)[KR:KR + MR, :, b * QB:(b + 1) * QB]
                    dve.wait_ge(max_row0, n + 1)
                    dve.tensor_copy(rows[:, 1:HG, :], rows[:, 0:1, :].broadcast_to([MR, HG - 1, QB]))\
                        .then_inc(max_rows, 1)
                if ev[0] == "turn_heads":
                    n = ev[1]
                    g, b = divmod(n, NB)
                    dve.wait_ge(misc_done, misc_use[ev] + 1)
                    o = bank[MISC_BANK][:, :].rearrange("p (t h c) -> p t h c", t=TB, h=HG)
                    inv = inv_sum[:, :].rearrange("p (t h) -> p t h", t=TB)
                    link(dve.reciprocal(inv, o[:, :, :, HD]))
                    to = heads[:, b * TB:(b + 1) * TB, g * HG * HD:(g + 1) * HG * HD]
                    dve.tensor_tensor(to.rearrange("p t (h i) -> p t h i", h=HG), o[:, :, :, 0:HD],
                                      inv.rearrange("p t (h i) -> p t h i", i=1).broadcast_to([P, TB, HG, HD]), ALU.mult)\
                        .then_inc(misc_read_v, 1)
                if ev[0] == "out":
                    after_projection(ev[1])
                if ev[0] == "rank":
                    choose(0 if ev[1] == 0 else 1, ev[1], ev[2])

            def split_weights(e, c):
                dve.wait_ge(w_high, CH * e + c + 1)
                dve.tensor_tensor(chunk(w_split[e % 2][:, 1, :], c), chunk(w_raw[:, e % 2, :], c),
                                  chunk(w_split[e % 2][:, 0, :], c).bitcast(F32), ALU.subtract).then_inc(w_ready, 1)

            def split_slots(e, ft):
                k = e * DT + ft
                dve.wait_ge(slotT_high, k + 1)
                dve.tensor_scalar(slotT_raw[:, ft, :], bank[SLOT_BANKS[ft]][:, 0:CAP], mod_col[:, 3, ft:ft + 1],
                                  mod_col[:, 2, ft:ft + 1], ALU.mult, ALU.add).then_inc(slotT_raw_done, 1)
                dve.wait_ge(slotT_raw_done, k + 1)
                dve.tensor_tensor(slotT[:, e % 2, 1, ft, :], slotT_raw[:, ft, :],
                                  slotT[:, e % 2, 0, ft, :].bitcast(F32), ALU.subtract).then_inc(slotT_ready, 1)

            def finish_rows(e):
                if e >= 2:
                    dve.wait_ge(rows_stored[e % 2], 16 * CT3 * (e // 2))
                for st in range(CT3):
                    k = CT3 * e + st
                    r = slice(0, rows_of(st))
                    dve.wait_ge(down_done, k + 1)
                    dve.scalar_tensor_tensor(out=down[r, e % 2, st, :], in0=bank[DOWN_BANKS[st]][r, 0:D],
                                             scalar=slots_sb[r, e % SR, st, 2 * D:2 * D + 1], in1=gates[r, 1, :],
                                             op0=ALU.mult, op1=ALU.mult).then_inc(down_read, 1)

            def add_rows(e, st):
                r = slice(0, rows_of(st))
                dve.wait_ge(down_read, CT3 * e + st + 1)
                dve.tensor_tensor(down[r, e % 2, st, :], down[r, e % 2, st, :], slots_sb[r, e % SR, st, 0:D],
                                  ALU.add).then_inc(rows_ready, 1)

            ADD_AT = (DOWN_LAG - 1, IT - 2, IT - 1)
            dve.memset(acts[:, :, :, CAP:CAPW].bitcast(F32), 0.0).then_inc(pads_zeroed, 1)
            for c in range(CH):
                split_weights(0, c)
            for ft in range(DT):
                split_slots(0, ft)
            for n in range(E * IT):
                e, it = divmod(n, IT)
                dve.wait_ge(gelu_done, n + 1)
                dve.tensor_tensor(acts[:, n % AR, 1, 0:CAP], act_raw[:, n % 2, :], acts[:, n % AR, 0, 0:CAP].bitcast(F32),
                                  ALU.subtract).then_inc(act_ready, 1)
                if it == DOWN_LAG - 1 and e >= 1:
                    finish_rows(e - 1)
                if it in ADD_AT and e >= 1:
                    add_rows(e - 1, ADD_AT.index(it))
                if e + 1 < E:
                    if 2 <= it < 2 + CH:
                        split_weights(e + 1, it - 2)
                    if it >= IT - DT:
                        split_slots(e + 1, it - (IT - DT))
            finish_rows(E - 1)
            for st in range(CT3):
                add_rows(E - 1, st)

        @block.tensor
        def _(pe):
            pe.wait_ge(pool_consts, 1)
            pe.wait_ge(silu_ready, 1)
            pe.wait_ge(loaded_shift, 32)

            def column_mods(pairs):
                for j, m in pairs:
                    for ft in range(DT):
                        for k in range(DT):
                            mm = pe.matmul(bank[2][:, j * DT + ft:j * DT + ft + 1],
                                           w_mod_sb[:, k, m * D + ft * P:m * D + (ft + 1) * P], silu[:, k:k + 1],
                                           start=(k == 0), stop=(k == DT - 1))
                return mm
            pe.matmul(bank[1][:, :], ones_f[0:1, :], bias_row.rearrange("a t d -> a (t d)"), start=True, stop=True)
            column_mods(((0, 0), (1, 1))).then_inc(mods_done, 1)

            def misc_free(ev):
                a, v = misc_reads(misc_use[ev])
                if a:
                    pe.wait_ge(misc_read_a, a)
                if v:
                    pe.wait_ge(misc_read_v, v)

            def project(g, b):
                misc_free(("project", g, b))
                for k in range(DT):
                    mm = pe.matmul(bank[MISC_BANK][:, :], w_qk_sb[:, k, g * P:(g + 1) * P],
                                   hT[:, k, b * QB:(b + 1) * QB], start=(k == 0), stop=(k == DT - 1))
                mm.then_inc(misc_done, 1)

            def prepare(b):
                pe.wait_ge(xhat_ready, (b + 1) * TB)
                if b >= 1:
                    pe.wait_ge(hT_ready, b * DT)
                for ft in range(DT):
                    for t in range(TB):
                        mm = pe.transpose(bank[TURN_BANKS[ft]][:, t * P:(t + 1) * P],
                                          xhat[:, (b * TB + t) % (2 * TB), ft * P:(ft + 1) * P], ident[:, :])
                    mm.then_inc(xhat_turned, 1)
                if b == 0:
                    pe.wait_ge(loaded_qkv, 48)
                pe.wait_ge(hT_ready, (b + 1) * DT)
                project(0, b)
                for t in range(b * TB, (b + 1) * TB):
                    if t >= 2:
                        pe.wait_ge(v_read, t - 1)
                    for k in range(DT):
                        mm = pe.matmul(bank[V_BANKS[t % 2]][:, 0:D], hT[:, k, t * P:(t + 1) * P], w_v_sb[:, k, :],
                                       start=(k == 0), stop=(k == DT - 1))
                    mm.then_inc(v_done, 1)

            def turn_heads(n):
                pe.wait_ge(o_read, n + 1)
                misc_free(("turn_heads", n))
                if n == NG * NB - 1:
                    pe.wait_ge(logits_read, 1)
                for t in range(TB):
                    mm = pe.transpose(bank[MISC_BANK][:, t * P:(t + 1) * P], o_sb[:, n % 2, t * P:(t + 1) * P], ident[:, :])
                mm.then_inc(misc_done, 1)

            def weigh_values(n, kt):
                s = step_of[n, kt]
                j = kt - (n % NB) * TB
                if j >= 0:
                    pe.wait_ge(diag_done, n * TB + j + 1)
                else:
                    pe.wait_ge(exp_done, HG * (s + 1))
                first, last = kt == key_tiles(n % NB)[0], kt == key_tiles(n % NB)[-1]
                if first and n >= 1:
                    pe.wait_ge(o_read, n)
                lo = P * max(0, j)
                g = n // NB
                for h in range(HG):
                    mm = pe.matmul(bank[VALUE_BANK][CT * h:CT * (h + 1), lo:QB], v_sb[:, kt, g * HG + h, :],
                                   probs[:, s % 3, h, 0:QB - lo], start=first, stop=last,
                                   skip_group_check=True)
                mm.then_inc(weighted, 1)

            def emptied(ready, t, times=1):
                last = t if t <= TAIL_TILES else t - 1
                if last:
                    pe.wait_ge(ready, times * last)

            for ev in plan:
                if ev[0] == "prepare":
                    prepare(ev[1])
                    if ev[1] == 0:
                        pe.wait_ge(loaded_mod, 16)
                        pe.wait_ge(silu_ready, 2)
                        pe.wait_ge(mods_read, 2)
                        column_mods(((2, 3), (3, 4)))
                        for j, m in enumerate((2, 5)):
                            for k in range(DT):
                                mm = pe.matmul(bank[0][:, j * D:(j + 1) * D], silu_rep[:, k, :],
                                               w_mod_sb[:, k, m * D:(m + 1) * D], start=(k == 0), stop=(k == DT - 1))
                        mm.then_inc(mods_done, 1)
                if ev[0] == "max":
                    _, u, g, b, qt, h, c, width = ev
                    if u == 0:
                        pe.wait_ge(mods_read, 4)
                    if (qt, h, c) == (0, 0, 0):
                        if g == 0:
                            pe.wait_ge(stacked_first[b], 16 * STACK_DMAS)
                        elif b == 0:
                            pe.wait_ge(stacked[g], 16 * STACK_DMAS)
                    if u >= 3:
                        pe.wait_ge(max_read, u - 2)
                    q0 = b * QB + qt * P
                    pe.matmul(bank[MAX_BANKS[u % 3]][:, 0:width], stack(g, 0)[0:KR, h, q0:q0 + P],
                              stack(g, 1)[0:KR, h, c * QB:c * QB + width], start=True, stop=True).then_inc(max_scored, 1)
                if ev[0] == "max_rows":
                    n = ev[1]
                    pe.wait_ge(max_parts, n + 1)
                    misc_free(ev)
                    for t in range(TB):
                        mm = pe.transpose(bank[MISC_BANK][:, :].bitcast(BF16)[0:MR, t * P:(t + 1) * P],
                                          max_part[:, n % 2, t * HG:(t + 1) * HG, :].rearrange("p h a -> p (h a)"),
                                          ident_b[:, :])
                    mm.then_inc(misc_done, 1)
                if ev[0] == "project":
                    project(ev[1], ev[2])
                if ev[0] == "scores":
                    _, n, kt, h = ev
                    g, b = divmod(n, NB)
                    u = HG * step_of[n, kt] + h
                    lo = P * max(0, kt - b * TB)
                    if kt == key_tiles(b)[0] and h == 0:
                        pe.wait_ge(max_rows, n + 1)
                        if n == 0:
                            pe.wait_ge(hT_ready, NB * DT)
                            pe.wait_ge(v_read, NT)
                        if b == 0 and g < 2:
                            pe.wait_ge(ones_rows, g + 1)
                    if u >= 3:
                        pe.wait_ge(exp_done, u - 2)
                    pe.matmul(bank[SCORE_BANKS[u % 3]][:, 0:QB - lo], stack(g, 1)[0:KR + MR, h, kt * P:(kt + 1) * P],
                              stack(g, 0)[0:KR + MR, h, b * QB + lo:(b + 1) * QB], start=True, stop=True)\
                        .then_inc(scored, 1)
                if ev[0] == "weigh":
                    weigh_values(ev[1], ev[2])
                if ev[0] == "turn_heads":
                    turn_heads(ev[1])
                if ev[0] == "turn":
                    t = ev[1]
                    if t == 0:
                        pe.wait_ge(max_read, units_before[-1])
                    emptied(oT_ready, t)
                    pe.wait_ge(misc_read_v, (NG - 1) * NB + t // TB + 1)
                    for ft in range(DT):
                        mm = pe.transpose(bank[tail_bank(0, t)][:, ft * P:(ft + 1) * P], heads[:, t, ft * P:(ft + 1) * P],
                                          ident[:, :])
                    mm.then_inc(heads_turned, 1)
                if ev[0] == "out":
                    t = ev[1]
                    if t == 0:
                        pe.wait_ge(loaded_late, 32)
                    emptied(x1_ready, t)
                    pe.wait_ge(oT_ready, t + 1)
                    for k in range(DT):
                        mm = pe.matmul(bank[tail_bank(1, t)][:, 0:D], oT_sb[:, t % 2, k * P:(k + 1) * P], w_o_sb[:, k, :],
                                       start=(k == 0), stop=(k == DT - 1))
                    mm.then_inc(projected, 1)
                if ev[0] == "turn_normal":
                    t = ev[1]
                    if t == TAIL_TILES:
                        pe.wait_ge(counts_read, 1)
                    emptied(h2T_ready, t, DT)
                    pe.wait_ge(xhat2_ready, t + 1)
                    for ft in range(DT):
                        mm = pe.transpose(bank[tail_bank(2, t)][:, ft * P:(ft + 1) * P], heads[:, t, ft * P:(ft + 1) * P],
                                          ident[:, :])
                    mm.then_inc(xhat2_turned, 1)
                if ev[0] == "gate":
                    t = ev[1]
                    if t == 0 or t == TAIL_TILES:
                        pe.wait_ge(misc_read_v, NG * NB - (1 if t == 0 else 0))
                    pe.wait_ge(h2T_ready, DT * (t + 1))
                    for k in range(DT):
                        mm = pe.matmul(bank[MISC_BANK][:, t * E:(t + 1) * E], h2T[:, t % 2, k * P:(k + 1) * P],
                                       w_gate_sb[:, k, :], start=(k == 0), stop=(k == DT - 1))
                    mm.then_inc(gated, 1)
                if ev[0] == "rank":
                    _, t0, t1 = ev
                    pe.wait_ge(onehot_ready, 1 if t0 == 0 else 2)
                    pe.wait_ge(h2T_ready, DT * t1)
                    chosen = onehot_b[:, t0:t1, :].rearrange("p t e -> p (t e)")
                    for i, w in enumerate((upper, ones_b)):
                        mm = pe.matmul(bank[COUNT_BANK][:, i * NT * E:i * NT * E + (t1 - t0) * E], w[:, :], chosen,
                                       start=True, stop=True)
                    mm.then_inc(counted, 1)

            def turn_slots(e):
                pe.wait_ge(slots_loaded[e % SR], 32 * (e // SR + 1))
                if e >= 1:
                    pe.wait_ge(slotT_high, DT * e)
                    pe.wait_ge(slotT_raw_done, DT * e)
                for ft in range(DT):
                    for st in range(CT3):
                        rows = rows_of(st)
                        mm = pe.transpose(bank[SLOT_BANKS[ft]][:, st * P:st * P + rows],
                                          slots_sb[0:rows, e % SR, st, D + ft * P:D + (ft + 1) * P], ident[0:rows, 0:rows])
                    mm.then_inc(slots_turned, 1)

            PAIRS = ((1, 0), (0, 1), (0, 0))

            def up(n):
                e, it = divmod(n, IT)
                if it == 0:
                    pe.wait_ge(w_ready, CH * e + CH // 2)
                    pe.wait_ge(slotT_ready, DT * (e + 1))
                if n >= 3:
                    pe.wait_ge(gelu_done, n - 2)
                for i, (a, b) in enumerate(PAIRS):
                    for k in range(DT):
                        col = k * I + it * P
                        mm = pe.matmul(bank[n % 3][:, 0:CAP], w_split[e % 2][:, a, col:col + P],
                                       slotT[:, e % 2, b, k, :], start=(i == 0 and k == 0),
                                       stop=(i == len(PAIRS) - 1 and k == DT - 1))
                mm.then_inc(up_done, 1)

            def down_to(n):
                e, it = divmod(n, IT)
                if it == 0:
                    pe.wait_ge(w_ready, CH * (e + 1))
                if n == 0:
                    pe.wait_ge(pads_zeroed, 1)
                pe.wait_ge(act_ready, n + 1)
                col = DT * I + it * D
                for st in range(CT3):
                    if it == 0 and e >= 1:
                        pe.wait_ge(down_read, CT3 * (e - 1) + st + 1)
                    for i, (a, b) in enumerate(PAIRS):
                        mm = pe.matmul(bank[DOWN_BANKS[st]][:, 0:D], acts[:, n % AR, a, st * P:(st + 1) * P],
                                       w_split[e % 2][:, b, col:col + D], start=(it == 0 and i == 0),
                                       stop=(it == IT - 1 and i == len(PAIRS) - 1))
                    if it == IT - 1:
                        mm.then_inc(down_done, 1)
                if it < IT - 1:
                    mm.then_inc(act_used, 1)

            pe.wait_ge(slots_known, 2)
            turn_slots(0)
            for n in range(E * IT):
                up(n)
                if n % IT == 4 and n // IT + 1 < E:
                    turn_slots(n // IT + 1)
                if n >= DOWN_LAG:
                    down_to(n - DOWN_LAG)
            for n in range(E * IT - DOWN_LAG, E * IT):
                down_to(n)


def kernel(L0_attn_x, L0_attn_w_qkv, L0_attn_b_qkv, L0_attn_w_out, L0_attn_b_out, L0_ffn_gate_weight, L0_ffn_wi,
           L0_ffn_wo, L0_c, L0_wmod):
    import numpy as np
    import concourse.bacc as bacc
    from concourse.bass_utils import run_bass_kernel_spmd

    w_qkv, b_qkv = np.asarray(L0_attn_w_qkv), np.asarray(L0_attn_b_qkv)
    q, k = (w_qkv[i * D:(i + 1) * D].reshape(NG, HG * HD, D) for i in range(2))
    bq, bk = (b_qkv[i * D:(i + 1) * D].reshape(NG, HG * HD) for i in range(2))
    arrays = {
        "x": np.asarray(L0_attn_x)[0],
        "w_qk": np.concatenate([q, k], axis=1).reshape(NG * P, D).T,
        "b_qk": np.concatenate([bq, bk], axis=1).T,
        "w_v": w_qkv[2 * D:].T,
        "w_o": np.asarray(L0_attn_w_out).T,
        "b_rows": np.stack([b_qkv[2 * D:], np.asarray(L0_attn_b_out)]),
        "w_gate": np.asarray(L0_ffn_gate_weight).T,
        "w_in": np.asarray(L0_ffn_wi),
        "w_down": np.asarray(L0_ffn_wo),
        "c_col": np.asarray(L0_c)[0].reshape(DT, P).T,
        "w_mod": np.asarray(L0_wmod),
    }
    arrays = {n: np.ascontiguousarray(a) for n, a in arrays.items()}
    nc = bacc.Bacc("TRN2", target_bir_lowering=False, num_devices=1)
    args = {n: nc.dram_tensor(n, a.shape, mybir.dt.from_np(a.dtype), kind="ExternalInput").ap()
            for n, a in arrays.items()}
    result = nc.dram_tensor("out", (S, D), F32, kind="ExternalOutput").ap()
    layer(nc, *args.values(), result)
    r = run_bass_kernel_spmd(nc, [arrays], core_ids=[0])
    return r.results[0]["out"].reshape(1, S, D)
```

```python
from contextlib import ExitStack

import concourse.bass as bass
from concourse import mybir

F32 = mybir.dt.float32
BF16 = mybir.dt.bfloat16
F32R = mybir.dt.float32r
U32 = mybir.dt.uint32
I32 = mybir.dt.int32
ALU = mybir.AluOpType
ACT = mybir.ActivationFunctionType
AX = mybir.AxisListType

P = 128
D = 256
DT = D // P
S = 2048
NT = S // P
QB = 512
TB = QB // P
NB = S // QB
H = 16
HD = D // H
HG = 4
NG = H // HG
CT = 32
PARTS_Q = [0, 0, 0, 1, 1, 2]
PARTS_K = [0, 1, 2, 0, 1, 0]
KR = HD * len(PARTS_Q)
MR = 2 * HG
SCALE = HD ** -0.5
NEG = -3.0e38
E = 8
I = 1024
IT = I // P
CAP = 320
NS = E * CAP
ROW = 2 * D + 2
CT3 = -(-CAP // P)
CAPW = CT3 * P
LAST_ROWS = CAP - (CT3 - 1) * P
BIAS_FROM = (NG - 2) * NB
DOWN_LAG = 2
TAIL_TILES = (NB - 1) * TB
RSQRT_SEED = float(0x5F3759DF)
EPS = 1e-5


def block_units():
    return [[(qt, h, c) for qt in range(TB) for h in range(HG) for c in range(b + 1)] for b in range(NB)]


TENSOR_RATE, VECTOR_RATE, SCALAR_RATE = 2.4, 0.96, 1.2
VECTOR_FIXED, SCALAR_FIXED, MASK_TIME = 75, 60, 700
SPLIT_LAG = 2500
SPLIT_TIME, STACK_TIME = 5000, 20000
PIECES = 4
PROJECT_FROM = {1: 0, 2: 1, 3: 6}
AHEAD_OF_ROWS, AHEAD_OF_SCORES = 2, 3


def key_tiles(b):
    diag, full = [b * TB + j for j in range(TB)], list(range(b * TB))
    order = []
    for j in range(TB):
        order += [diag[j]] + full[j:j + 1]
    return order + full[TB:]


TAIL_LAG = TB + 2


def tail_slot(k, t0, t1):
    stages = (("turn", k), ("out", k - 1), ("turn_normal", k - TAIL_LAG), ("gate", k - TAIL_LAG - 1))
    return [ev for ev in stages if t0 <= ev[1] < t1]


PROLOGUE_1 = [("normal", 0), ("turn_x", 0), ("normal", 1), ("first_qk", 0), ("turn_x", 1), ("values", 0), ("normal", 2),
              ("first_qk", 1), ("values", 1)]
PROLOGUE_2 = [("turn_x", 2), ("normal", 3), ("first_qk", 2), ("turn_x", 3), ("values", 2), ("first_qk", 3), ("values", 3),
              ("mods",), ("gate_bias",)]


def attention_plan():
    units = block_units()
    maxima = [(g, b, u) for g in range(NG) for b in range(NB) for u in range(len(units[b]))]
    plan = []
    now = 0.0
    vector = []
    scalar = []
    block = 0
    projections = [(g, b) for g in range(1, NG) for b in range(NB)]
    projected = -1e9
    split = None
    parts_at = {}
    scored_at = {-1: 0.0}
    placed_at = {}
    waiting_rows = []

    def tensor(ns, after=0.0):
        nonlocal now
        now = max(now, after) + ns

    def bank_free(read):
        return read[-3] if len(read) >= 3 else 0.0

    def read_by(read, rate, fixed, width, latency=60):
        read.append(max(read[-1] if read else 0.0, now + latency) + width / rate + fixed)

    def emit_max():
        g, b, u = maxima[len(vector)]
        qt, h, c = units[b][u]
        width = QB if c < b else P * (qt + 1)
        plan.append(("max", len(vector), g, b, qt, h, c, width))
        tensor(width / TENSOR_RATE + 3, bank_free(vector))
        read_by(vector, VECTOR_RATE, VECTOR_FIXED, width)
        if u == len(units[b]) - 1:
            n = g * NB + b
            turn_rows(all_of=n - 2)
            plan.append(("max_parts", n))
            vector[-1] += 400
            waiting_rows.append([n, vector[-1] + 100])

    def turn_rows(all_of=-1):
        while waiting_rows and (waiting_rows[0][1] <= now or waiting_rows[0][0] <= all_of):
            n, formed = waiting_rows.pop(0)
            plan.append(("max_rows", n))
            tensor(300, formed)
            placed_at[n] = now + 1700
            vector[-1] = max(vector[-1], now + 550) + 450

    def may_run():
        if len(vector) == len(maxima):
            return False
        g, b, u = maxima[len(vector)]
        if g <= block // NB:
            return True
        return (g in parts_at and g - 2 in scored_at
                and now >= max(parts_at[g], scored_at[g - 2]) + STACK_TIME)

    def last_of_block():
        g, b, u = maxima[len(vector)]
        return u == len(units[b]) - 1

    def fill(until=0.0):
        while may_run() and bank_free(vector) <= max(now, until):
            emit_max()
        turn_rows()

    def may_go_beside(n, turned):
        if not beside or len(vector) < len(maxima):
            return False
        through = n - (NG - 1) * NB - (0 if turned else 1)
        if beside[0][0] == "turn":
            return beside[0][1] < TB * through
        return beside[0][0] != "gate" or through == NB - 1

    def run_ahead(count):
        for _ in range(count):
            if may_run() and not last_of_block():
                emit_max()

    def project():
        nonlocal split, projected
        if split and now >= projected + SPLIT_LAG:
            plan.append(("split", *split))
            split = None
        if projections and not split and block >= PROJECT_FROM[projections[0][0]] and now >= projected + SPLIT_TIME:
            split = projections.pop(0)
            for piece in range(PIECES):
                plan.append(("project", *split, piece))
                tensor(1720 / PIECES)
                if piece < PIECES - 1 and may_run() and bank_free(vector) <= now and not last_of_block():
                    emit_max()
            projected = now
            if split[1] == NB - 1:
                parts_at[split[0]] = now + SPLIT_TIME

    weigh = None
    beside = [ev for k in range(TAIL_TILES + TAIL_LAG + 1) for ev in tail_slot(k, 0, TAIL_TILES)]
    beside += [("rank", 0, TAIL_TILES), ("scores_only",), ("scores_only",), ("scores_only",), ("scores_only",),
               ("gate_exp", 0, TAIL_TILES)]
    plan += PROLOGUE_1
    while maxima[len(vector)][:2] == (0, 0):
        emit_max()
    plan += PROLOGUE_2
    now += 12000
    for n in range(NG * NB):
        g, b = divmod(n, NB)
        block = n
        if b == 0:
            scored_at[g - 1] = now
        while len(vector) < len(maxima) and maxima[len(vector)][0] * NB + maxima[len(vector)][1] <= n:
            emit_max()
            turn_rows()
            project()
        if waiting_rows and waiting_rows[0][0] <= n:
            run_ahead(AHEAD_OF_ROWS)
            turn_rows(all_of=n)
            run_ahead(AHEAD_OF_SCORES)
        for i, kt in enumerate(key_tiles(b)):
            width = QB - P * max(0, kt - b * TB)
            for h in range(HG):
                fill(bank_free(scalar))
                plan.append(("scores", n, kt, h))
                tensor(width / TENSOR_RATE + 3, max(bank_free(scalar), placed_at[n]))
                read_by(scalar, SCALAR_RATE, SCALAR_FIXED, width)
                if may_go_beside(n, (i, h) > (1, 1)) and not (n == NG * NB - 1 and h == HG - 1):
                    plan.append(beside.pop(0))
                    tensor(450)
                if h == 1 and n >= 1 and i == 1:
                    plan.append(("turn_heads", n - 1))
                    tensor(500)
                    if vector:
                        vector[-1] = max(vector[-1], now + 60) + 550
            if weigh is not None:
                fill(weigh[3])
                plan.append(("weigh", weigh[0], weigh[1]))
                tensor(HG * weigh[2] * 234 / QB, weigh[3])
                if weigh[0] < n:
                    plan.append(("heads_out", n - 1))
                    scalar[-1] = max(scalar[-1], now + 60) + 480
            weigh = (n, kt, width, scalar[-1] + 60 + (MASK_TIME if kt >= b * TB else 0))
            project()
    plan += beside
    plan.append(("weigh", weigh[0], weigh[1]))
    plan.append(("heads_out", weigh[0]))
    plan.append(("turn_heads", weigh[0]))
    for k in range(TAIL_TILES, NT + TAIL_LAG + 1):
        plan.extend(tail_slot(k, TAIL_TILES, NT))
    plan.append(("rank", TAIL_TILES, NT))
    plan.append(("gate_exp", TAIL_TILES, NT))
    return plan


def layer(nc, x, w_qk, b_qk, w_v, w_o, b_rows, w_gate, w_in, w_down, c_col, w_mod, out):
    qk_rows = nc.dram_tensor("qk_rows", (2, 2, len(PARTS_Q), P // 2, S), BF16, kind="Internal").ap()
    slot_rows = nc.dram_tensor("slot_rows", (NS, ROW), F32, kind="Internal").ap()

    plan = attention_plan()
    misc_use = {}
    for ev in plan:
        if ev[0] == "first_qk":
            misc_use["project", 0, ev[1]] = len(misc_use)
        if ev[0] == "project" and ev[3] == 0:
            misc_use[ev[:3]] = len(misc_use)
        if ev[0] in ("max_rows", "turn_heads", "gate_bias"):
            misc_use[ev] = len(misc_use)

    with ExitStack() as ctx:
        def sem(name):
            return ctx.enter_context(nc.semaphore(name))

        def sb(name, shape, dt):
            return ctx.enter_context(nc.sbuf_tensor(name, shape, dt))

        bank = [ctx.enter_context(nc.psum_tensor(f"bank{i}", [P, QB], F32)) for i in range(8)]
        MAX_BANKS, SCORE_BANKS, VALUE_BANK, MISC_BANK = (0, 1, 2), (3, 4, 5), 6, 7
        TURN_BANKS, V_BANKS = (3, 4), (5, 6)
        COUNT_BANK = 2
        DOWN_BANKS, SLOT_BANKS = (3, 4, 5), (6, 7)

        def tail_bank(stage, t):
            return stage + (3 if t >= TAIL_TILES and t % 2 else 0)

        token = sb("token", [P, NT, ROW], F32)
        x_sb = token[:, :, 0:D]
        heads = token[:, :, D:2 * D]
        prob = token[:, :, 2 * D]
        token_id = token[:, :, 2 * D + 1:ROW]
        w_o_sb = sb("w_o_sb", [P, DT, D], F32)
        w_gate_sb = sb("w_gate_sb", [P, DT, E], F32)
        gates = sb("gates", [P, 2, D], F32)
        mod_col = sb("mod_col", [P, 4, DT], F32)
        ident = sb("ident", [P, P], F32)
        stats = sb("stats", [P, NT, 6], F32)
        mean_var = sb("mean_var", [P, NT, 2], F32)
        root = sb("root", [P, 2, NT], F32)
        rstd = sb("rstd", [P, NT], F32)
        product = sb("product", [P, 2, D], F32)
        logits = sb("logits", [P, NT, E], F32)
        expd = sb("expd", [P, NT, E], F32)
        top = sb("top", [P, NT], F32)
        onehot = sb("onehot", [P, NT, E], F32)
        onehot_b = sb("onehot_b", [P, NT, E], BF16)
        order = sb("order", [P, NT, E], F32)
        limit = sb("limit", [P, NT, E], F32)
        earlier = sb("earlier", [P, NT + 1, E], F32)
        gate_bias = sb("gate_bias", [P, E], F32)
        before = sb("before", [P, NT, E], F32)
        slot_limit = sb("slot_limit", [P, NT], F32)
        over = sb("over", [P, NT], F32)
        slot = sb("slot", [P, NT], F32)
        slot_to = sb("slot_to", [P, NT], U32)
        upper = sb("upper", [P, P], BF16)
        ones_b = sb("ones_b", [P, P], BF16)
        empty = sb("empty", [P, ROW], F32)
        attention = ExitStack()

        def sb1(name, shape, dt):
            return attention.enter_context(nc.sbuf_tensor(name, shape, dt))
        stacks = sb1("stacks", [P, 2, 2, HG, S], BF16)
        hT = sb1("hT", [P, DT, S], F32)
        v_sb = sb1("v_sb", [P, NT, H, CT], F32)
        probs = sb1("probs", [P, 3, HG, QB], F32)
        early = probs[:, :, :, :].rearrange("p a b c -> p (a b c)")
        w_mod_sb = early[:, 0:DT * 6 * D].rearrange("p (t n) -> p t n", t=DT)
        silu_rep = early[:, DT * 6 * D:DT * 6 * D + DT * P].rearrange("p (t n) -> p t n", t=DT)
        at = DT * 6 * D + DT * P
        xhat = early[:, at:at + 2 * TB * D].rearrange("p (t d) -> p t d", d=D)
        bias_row = early[0:1, at + 2 * TB * D:at + (2 * TB + 2) * D].rearrange("p (a d) -> p a d", a=2)
        bias_all = sb1("bias_all", [P, 2, D], F32)
        ident_b = sb1("ident_b", [P, P], BF16)
        ones_f = sb1("ones_f", [P, P], F32)
        w_qk_sb = sb1("w_qk_sb", [P, DT, NG * P], F32)
        w_v_sb = sb1("w_v_sb", [P, DT, D], F32)
        qk_sb = sb1("qk_sb", [P, QB], F32)
        rest = sb1("rest", [P, QB], F32)
        oT_sb = qk_sb[:, :].rearrange("p (r n) -> p r n", r=2)
        xhat2T = rest[:, :].rearrange("p (r n) -> p r n", r=2)
        part = sb1("part", [P, 3, QB], BF16)
        b_qk_sb = sb1("b_qk_sb", [P, NG], F32)
        qk_scale = sb1("qk_scale", [P, 1], F32)
        c_sb = sb1("c_sb", [P, DT], F32)
        c_tmp = sb1("c_tmp", [P, 3, DT], F32)
        silu = sb1("silu", [P, DT], F32)
        sign = product
        causal = sb1("causal", [P, QB], F32)
        masked = sb1("masked", [P, 3, QB], BF16)
        head_sel = sb1("head_sel", [P, HG], F32)
        chunk_max = sb1("chunk_max", [P, 2, TB * HG, NB], F32)
        neg_max = sb1("neg_max", [P, TB * HG], F32)
        max_part = sb1("max_part", [P, 2, TB * HG, 2], BF16)
        o_sb = sb1("o_sb", [P, 2, QB], F32)
        inv_sum = sb1("inv_sum", [P, TB * HG], F32)
        attention.close()
        WN = 2 * DT * I
        w_raw = sb("w_raw", [P, 2, WN], F32)
        w_split = [sb("w_split0", [P, 2, WN], F32R)]
        w_split.append(sb("w_split1", [P, 2, WN], F32R))
        SR = 4
        slots_sb = sb("slots_sb", [P, SR, CT3, ROW], F32)
        slotT = sb("slotT", [P, 2, 2, DT, CAP], F32R)
        slotT_raw = sb("slotT_raw", [P, DT, CAP], F32)
        act_raw = sb("act_raw", [P, 2, CAP], F32)
        AR = 3
        acts = sb("acts", [P, AR, 2, CAPW], F32R)
        down = sb("down", [P, 2, CT3, D], F32)

        loaded_c = sem("loaded_c")
        loaded_shift = sem("loaded_shift")
        loaded_mod = sem("loaded_mod")
        loaded_x = [sem(f"loaded_x{b}") for b in range(NB)]
        loaded_qkv = sem("loaded_qkv")
        loaded_late = sem("loaded_late")
        pool_consts = sem("pool_consts")
        pool_chain = sem("pool_chain")
        v_zeroed = sem("v_zeroed")
        c_exp = sem("c_exp")
        silu_ready = sem("silu_ready")
        mods_done = sem("mods_done")
        mods_read = sem("mods_read")
        dve_chain = sem("dve_chain")
        xhat_ready = sem("xhat_ready")
        xhat_turned = sem("xhat_turned")
        hT_ready = sem("hT_ready")
        v_done = sem("v_done")
        v_read = sem("v_read")
        w_o_ready = sem("w_o_ready")
        gate_rows_ready = sem("gate_rows_ready")
        w_gate_ready = sem("w_gate_ready")
        x_biased = sem("x_biased")
        misc_done = sem("misc_done")
        misc_read_a = sem("misc_read_a")
        misc_read_v = sem("misc_read_v")
        part0_ready = sem("part0_ready")
        rest_ready_v = sem("rest_ready_v")
        rest_ready_p = sem("rest_ready_p")
        part1_ready = sem("part1_ready")
        qk_split_v = sem("qk_split_v")
        qk_split_p = sem("qk_split_p")
        parts_stored = sem("parts_stored")
        STACK_DMAS = 2
        STORES = 6
        stacked = [sem(f"stacked{g}") for g in range(NG)]
        stacked_first = [sem(f"stacked_first{b}") for b in range(NB)]
        ones_rows = sem("ones_rows")
        ones_copied = sem("ones_copied")
        max_scored = sem("max_scored")
        max_read = sem("max_read")
        max_parts = sem("max_parts")
        max_row0 = sem("max_row0")
        max_rows = sem("max_rows")
        scored = sem("scored")
        exp_done = sem("exp_done")
        diag_done = sem("diag_done")
        weighted = sem("weighted")
        o_read = sem("o_read")
        empty_ready = sem("empty_ready")
        causal_ready = sem("causal_ready")
        pads_zeroed = sem("pads_zeroed")
        slots_emptied = sem("slots_emptied")
        heads_turned = sem("heads_turned")
        oT_ready = sem("oT_ready")
        projected = sem("projected")
        x1_ready = sem("x1_ready")
        xhat2_ready = sem("xhat2_ready")
        xhat2_turned = sem("xhat2_turned")
        xhat2T_ready = sem("xhat2T_ready")
        gated = sem("gated")
        exp_gate = sem("exp_gate")
        top_ready = sem("top_ready")
        logits_read = sem("logits_read")
        onehot_ready = sem("onehot_ready")
        counted = sem("counted")
        counts_read = sem("counts_read")
        slots_known = sem("slots_known")
        scattered = sem("scattered")
        slots_loaded = [sem(f"slots_loaded{r}") for r in range(SR)]
        slots_turned = sem("slots_turned")
        slotT_high = sem("slotT_high")
        slotT_raw_done = sem("slotT_raw_done")
        slotT_ready = sem("slotT_ready")
        w_loaded = [sem(f"w_loaded{r}") for r in range(2)]
        w_high = sem("w_high")
        w_ready = sem("w_ready")
        up_done = sem("up_done")
        gelu_done = sem("gelu_done")
        act_ready = sem("act_ready")
        act_used = sem("act_used")
        down_done = sem("down_done")
        down_read = sem("down_read")
        rows_ready = sem("rows_ready")
        kept_stored = sem("kept_stored")
        rows_stored = [sem(f"rows_stored{r}") for r in range(2)]

        step_of = {}
        for n in range(NG * NB):
            for kt in key_tiles(n % NB):
                step_of[n, kt] = len(step_of)
        last_step = [step_of[n, key_tiles(n % NB)[-1]] for n in range(NG * NB)]
        units_before = [0]
        for g in range(NG):
            for u in block_units():
                units_before.append(units_before[-1] + len(u))

        def misc_reads(index):
            kinds = [k[0] for k, i in misc_use.items() if i < index]
            by_vector = sum(k in ("turn_heads", "gate_bias") for k in kinds)
            return len(kinds) - by_vector, by_vector

        def heads_read(n):
            return misc_reads(misc_use["turn_heads", n])[1] + 1

        def stack(g, side):
            return stacks[:, g % 2, side, :, :]

        CH = 4
        CW = WN // CH

        def chunk(w, c):
            return w[:, c * CW:(c + 1) * CW]

        block = ctx.enter_context(nc.Block())

        def load_expert(eng, e):
            w = w_raw[:, e % 2, :]
            eng.dma_start(w[:, 0:DT * I].rearrange("p (t n) -> p t n", t=DT),
                          w_in[e].rearrange("(t p) n -> p t n", p=P)).then_inc(w_loaded[e % 2], 16)
            eng.dma_start(w[:, DT * I:].rearrange("p (t n) -> p t n", t=IT),
                          w_down[e].rearrange("(t p) n -> p t n", p=P)).then_inc(w_loaded[e % 2], 16)

        def load_slots(eng, e):
            rows = slot_rows[e * CAP:(e + 1) * CAP, :]
            eng.dma_start(slots_sb[:, e % SR, 0:CT3 - 1, :],
                          rows[0:(CT3 - 1) * P, :].rearrange("(t p) d -> p t d", p=P)).then_inc(slots_loaded[e % SR], 16)
            eng.dma_start(slots_sb[0:LAST_ROWS, e % SR, CT3 - 1, :],
                          rows[(CT3 - 1) * P:CAP, :]).then_inc(slots_loaded[e % SR], 16)

        def rows_of(st):
            return min(P, CAP - st * P)

        @block.sync
        def _(sp):
            sp.dma_start(c_sb[:, :], c_col).then_inc(loaded_c, 16)
            sp.dma_start(x_sb[:, 0:TB, :], x[0:QB, :].rearrange("(t p) d -> p t d", p=P)).then_inc(loaded_x[0], 16)
            sp.dma_start(w_mod_sb[:, :, 0:2 * D], w_mod[:, 0:2 * D].rearrange("(t p) n -> p t n", p=P))\
              .then_inc(loaded_shift, 16)
            sp.dma_start(bias_row, b_rows.rearrange("(a t) d -> a t d", a=1)).then_inc(loaded_shift, 16)
            sp.dma_start(w_qk_sb[:, :, :], w_qk.rearrange("(t p) n -> p t n", p=P)).then_inc(loaded_qkv, 16)
            sp.dma_start(b_qk_sb[:, :], b_qk).then_inc(loaded_qkv, 16)
            sp.dma_start(w_v_sb[:, :, :], w_v.rearrange("(t p) n -> p t n", p=P)).then_inc(loaded_qkv, 16)
            for b in range(1, NB):
                sp.dma_start(x_sb[:, b * TB:(b + 1) * TB, :],
                             x[b * QB:(b + 1) * QB, :].rearrange("(t p) d -> p t d", p=P)).then_inc(loaded_x[b], 16)
                if b == 1:
                    sp.dma_start(w_mod_sb[:, :, 2 * D:], w_mod[:, 2 * D:].rearrange("(t p) n -> p t n", p=P))\
                      .then_inc(loaded_mod, 16)
            sp.dma_start(w_o_sb[:, :, :], w_o.rearrange("(t p) n -> p t n", p=P)).then_inc(loaded_late, 16)
            sp.dma_start(w_gate_sb[:, :, :], w_gate.rearrange("(t p) n -> p t n", p=P)).then_inc(loaded_late, 16)
            def run_of(p):
                first = PARTS_Q.index(p)
                return slice(first, first + PARTS_Q.count(p))

            def store_parts(g, b):
                n = g * NB + b
                cols = slice(b * QB, (b + 1) * QB)
                q_rows, k_rows = (qk_rows[g % 2, side, :, :, cols].rearrange("r p s -> p r s") for side in range(2))
                q, k = part[0:P // 2, :, :], part[P // 2:P, :, :]
                split_done, before_it = (qk_split_v, 0) if g == 0 else (qk_split_p, NB)
                for p in range(3):
                    sp.wait_ge((part0_ready, part1_ready, split_done)[p], n + 1 - (before_it if p == 2 else 0))
                    run = run_of(p)
                    sp.dma_start(q_rows[:, run, :], q[:, p:p + 1, :].broadcast_to([P // 2, run.stop - run.start, QB]))\
                      .then_inc(parts_stored, 16)
                    run = run_of(2 - p)
                    assert PARTS_K[run] == list(range(p + 1))
                    sp.dma_start(k_rows[:, run, :], k[:, 0:p + 1, :]).then_inc(parts_stored, 16)

            def load_stacks(g, cols, done):
                for side in range(2):
                    sp.dma_start(stack(g, side)[0:KR, :, cols],
                                 qk_rows[g % 2, side].rearrange("r (i h) s -> (r i) h s", h=HG)[:, :, cols])\
                      .then_inc(done, 16)

            for b in range(NB):
                store_parts(0, b)
                sp.wait_ge(parts_stored, 16 * STORES * (b + 1))
                load_stacks(0, slice(b * QB, (b + 1) * QB), stacked_first[b])
            for b in range(NB):
                sp.wait_ge(stacked_first[b], STACK_DMAS * 16)
            sp.wait_ge(ones_rows, HG)
            sp.dma_start(stacks[KR:KR + MR, 1, 1, :, :], stacks[KR:KR + MR, 0, 1, :, :]).then_inc(ones_copied, 16)
            for g in range(1, NG):
                if g >= 3:
                    sp.wait_ge(stacked[g - 2], 16 * STACK_DMAS)
                for b in range(NB):
                    store_parts(g, b)
                sp.wait_ge(parts_stored, 16 * STORES * NB * (g + 1))
                if g >= 2:
                    sp.wait_ge(scored, HG * (last_step[(g - 1) * NB - 1] + 1))
                load_stacks(g, slice(0, S), stacked[g])
            sp.wait_ge(empty_ready, 1)
            sp.dma_start(slot_rows.rearrange("(t p) d -> p t d", p=P),
                         empty[:, :].rearrange("p (t d) -> p t d", t=1).broadcast_to([P, NS // P, ROW]))\
              .then_inc(slots_emptied, 16)
            even = (NG - 1) * NB
            sp.wait_ge(scored, HG * (last_step[even - 1] + 1))
            sp.wait_ge(max_scored, units_before[even])
            for e in range(2):
                load_expert(sp, e)
            for b in range(NB):
                sp.wait_ge(x1_ready, (b + 1) * TB)
                sp.dma_start(out[b * QB:(b + 1) * QB, :].rearrange("(t p) d -> p t d", p=P),
                             x_sb[:, b * TB:(b + 1) * TB, :]).then_inc(kept_stored, 16)
            sp.wait_ge(scattered, 16 * NT)
            for e in range(SR):
                load_slots(sp, e)
            for e in range(E):
                if e >= 2:
                    sp.wait_ge(w_ready, CH * (e - 1))
                    load_expert(sp, e)
                if e >= SR:
                    f = e - SR
                    sp.wait_ge(rows_stored[f % 2], 16 * CT3 * (f // 2 + 1))
                    load_slots(sp, e)

        def leave_part0(eng, n, done):
            eng.wait_ge(part0_ready, n + 1)
            eng.tensor_tensor(rest[:, :], qk_sb[:, :], part[:, 0, :], ALU.subtract).then_inc(done, 1)

        def leave_part1(eng, n, done):
            eng.wait_ge(part1_ready, n + 1)
            eng.tensor_tensor(part[:, 2, :], rest[:, :], part[:, 1, :], ALU.subtract).then_inc(done, 1)

        @block.gpsimd
        def _(pool):
            chain = [0]

            def link(ins):
                chain[0] += 1
                ins.then_inc(pool_chain, 1)
                pool.wait_ge(pool_chain, chain[0])

            link(pool.memset(ones_f[:, :], 1.0))
            link(pool.memset(ones_b[:, :], 1.0))
            link(pool.memset(qk_scale[0:P // 2, :], SCALE))
            link(pool.memset(qk_scale[P // 2:P, :], 1.0))
            link(pool.memset(head_sel[:, :], 1.0))
            rows = head_sel[KR:KR + MR, :]
            link(pool.affine_select(out=rows, in_=rows, compare_op=ALU.is_ge, fill=0.0, base=0,
                                    pattern=[[-2, HG]], channel_multiplier=1))
            link(pool.affine_select(out=rows, in_=rows, compare_op=ALU.is_ge, fill=0.0, base=1,
                                    pattern=[[2, HG]], channel_multiplier=-1))
            link(pool.memset(ident[:, :], 0.0))
            link(pool.affine_select(out=ident[:, :], in_=ident[:, :], compare_op=ALU.not_equal, fill=1.0, base=0,
                                    pattern=[[-1, P]], channel_multiplier=1))
            link(pool.tensor_copy(ident_b[:, :], ident[:, :]))
            pool.memset(ones_f[0:1, 0:1], 1.0).then_inc(pool_consts, 1)
            link(pool.memset(v_sb[:, :, :, :], 0.0))
            pool.memset(v_sb[:, :, :, HD:HD + 1], 1.0).then_inc(v_zeroed, 1)
            link(pool.memset(causal[:, :], 0.0))
            pool.affine_select(out=causal[:, QB - P:QB], in_=causal[:, QB - P:QB], compare_op=ALU.is_ge,
                               fill=NEG, base=0, pattern=[[-1, P]], channel_multiplier=1).then_inc(causal_ready, 1)
            link(pool.affine_select(out=upper[:, :], in_=ones_b[:, :], compare_op=ALU.is_gt, fill=0.0, base=0,
                                    pattern=[[1, P]], channel_multiplier=-1))
            for e in range(E):
                pool.memset(order[:, :, e], float(E - e))
                pool.memset(earlier[:, 0, e:e + 1], float(CAP * e))
                last = pool.memset(limit[:, :, e], float(CAP * (e + 1)))
            link(last)
            link(pool.iota(token_id.bitcast(I32), pattern=[[P, NT]], base=0, channel_multiplier=1))
            link(pool.memset(empty[:, :], 0.0))
            pool.memset(empty[:, ROW - 1:ROW].bitcast(I32), S).then_inc(empty_ready, 1)

            biased = 0
            for ev in plan:
                if ev[0] == "project" and ev[3] == PIECES - 1:
                    leave_part0(pool, ev[1] * NB + ev[2], rest_ready_p)
                if ev[0] == "split":
                    leave_part1(pool, ev[1] * NB + ev[2], qk_split_p)
                if ev[0] == "scores" and ev[3] == HG - 1:
                    _, n, kt, h = ev
                    j = kt - (n % NB) * TB
                    if j >= 0:
                        s = step_of[n, kt]
                        pool.wait_ge(exp_done, HG * (s + 1))
                        d = probs[:, s % 3, :, 0:P]
                        pool.affine_select(out=d, in_=d, compare_op=ALU.is_ge, fill=0.0, base=0,
                                           pattern=[[0, HG], [1, P]], channel_multiplier=-1).then_inc(diag_done, 1)
                    if j >= 0 and BIAS_FROM <= n and biased < NT:
                        if biased == 0:
                            pool.wait_ge(mods_read, 4)
                            pool.wait_ge(xhat_ready, NT)
                            link(pool.tensor_tensor(product[:, 0, :], gates[:, 0, :], bias_all[:, 1, :], ALU.mult))
                            pool.wait_ge(loaded_late, 32)
                            for k in range(DT):
                                w_o_done = pool.tensor_tensor(w_o_sb[:, k, :], w_o_sb[:, k, :], gates[:, 0, :], ALU.mult)
                            w_o_done.then_inc(w_o_ready, 1)
                        pool.tensor_tensor(x_sb[:, biased, :], x_sb[:, biased, :], product[:, 0, :], ALU.add)\
                            .then_inc(x_biased, 1)
                        biased += 1
                if ev[0] == "rank":
                    _, t0, t1 = ev
                    if t0 == 0:
                        pool.wait_ge(slots_emptied, 16)
                    pool.wait_ge(slots_known, 1 if t0 == 0 else 2)
                    for t in range(t0, t1):
                        pool.indirect_dma_start(
                            out=slot_rows, out_offset=bass.IndirectOffsetOnAxis(ap=slot_to[:, t:t + 1], axis=0),
                            in_=token[:, t, :], in_offset=None, bounds_check=NS - 1, oob_is_err=False)\
                            .then_inc(scattered, 16)
            pool.wait_ge(kept_stored, 16 * NB)
            for e in range(E):
                for st in range(CT3):
                    rows = rows_of(st)
                    pool.wait_ge(rows_ready, CT3 * e + st + 1)
                    pool.indirect_dma_start(
                        out=out, out_offset=bass.IndirectOffsetOnAxis(
                            ap=slots_sb[0:rows, e % SR, st, ROW - 1:ROW].bitcast(U32), axis=0),
                        in_=down[0:rows, e % 2, st, :], in_offset=None, bounds_check=S - 1, oob_is_err=False)\
                        .then_inc(rows_stored[e % 2], 16)
            for r in range(2):
                pool.wait_ge(rows_stored[r], 16 * CT3 * E // 2)

        @block.scalar
        def _(act):
            act.wait_ge(loaded_c, 16)
            act.activation(c_tmp[:, 0, :], c_sb[:, :], ACT.Exp, scale=-1.0).then_inc(c_exp, 1)

            def read_projection(g, b):
                n = g * NB + b
                act.wait_ge(misc_done, misc_use["project", g, b] + 1)
                if n >= 1:
                    act.wait_ge(rest_ready_v if n <= NB else rest_ready_p, n if n <= NB else n - NB)
                act.activation(qk_sb[:, :], bank[MISC_BANK][:, :], ACT.Identity, bias=b_qk_sb[:, g:g + 1],
                               scale=qk_scale[:, 0:1]).then_inc(misc_read_a, 1)
                act.wait_ge(misc_read_a, misc_reads(misc_use["project", g, b])[0] + 1)
                if n >= 1:
                    act.wait_ge(parts_stored, 16 * STORES * n)
                act.copy(part[:, 0, :], qk_sb[:, :]).then_inc(part0_ready, 1)

            def second_part(g, b):
                n = g * NB + b
                act.wait_ge(rest_ready_v if g == 0 else rest_ready_p, n + 1 if g == 0 else n + 1 - NB)
                act.copy(part[:, 1, :], rest[:, :]).then_inc(part1_ready, 1)

            for ev in plan:
                if ev[0] == "turn_x":
                    b = ev[1]
                    if b == 0:
                        act.wait_ge(mods_read, 1)
                    for ft in range(DT):
                        act.wait_ge(xhat_turned, b * DT + ft + 1)
                        act.activation(hT[:, ft, b * QB:(b + 1) * QB], bank[TURN_BANKS[ft]][:, :], ACT.Identity,
                                       bias=mod_col[:, 0, ft:ft + 1], scale=mod_col[:, 1, ft:ft + 1]).then_inc(hT_ready, 1)
                if ev[0] == "first_qk":
                    b = ev[1]
                    if b == 0:
                        act.wait_ge(silu_ready, 2)
                    read_projection(0, b)
                    second_part(0, b)
                    act.activation(stacks[KR:KR + MR, 0, 1, b, :], ones_b[KR:KR + MR, 0:1].broadcast_to([MR, S]),
                                   ACT.Copy, scale=head_sel[KR:KR + MR, b:b + 1]).then_inc(ones_rows, 1)
                if ev[0] == "project" and ev[3] == PIECES - 1:
                    read_projection(ev[1], ev[2])
                if ev[0] == "split":
                    second_part(ev[1], ev[2])
                if ev[0] == "max_rows":
                    n = ev[1]
                    g, b = divmod(n, NB)
                    act.wait_ge(misc_done, misc_use[ev] + 1)
                    act.copy(stack(g, 0)[KR:KR + MR, 0, b * QB:(b + 1) * QB],
                             bank[MISC_BANK][:, :].bitcast(BF16)[0:MR, 0:QB]).then_inc(misc_read_a, 1)
                    act.wait_ge(misc_read_a, misc_reads(misc_use[ev])[0] + 1)
                    act.copy(c_tmp[0:1, 1, 0:1], c_tmp[0:1, 0, 0:1]).then_inc(max_row0, 1)
                if ev[0] == "scores":
                    _, n, kt, h = ev
                    s = step_of[n, kt]
                    u = HG * s + h
                    width = QB - P * max(0, kt - (n % NB) * TB)
                    act.wait_ge(scored, u + 1)
                    if h == 0 and s >= 3:
                        act.wait_ge(weighted, s - 2)
                    act.activation(probs[:, s % 3, h, 0:width], bank[SCORE_BANKS[u % 3]][:, 0:width], ACT.Exp)\
                        .then_inc(exp_done, 1)
                if ev[0] == "heads_out":
                    n = ev[1]
                    act.wait_ge(weighted, last_step[n] + 1)
                    if n >= 2:
                        act.wait_ge(misc_done, misc_use["turn_heads", n - 2] + 1)
                    act.copy(o_sb[:, n % 2, :], bank[VALUE_BANK][:, :]).then_inc(o_read, 1)
                if ev[0] == "turn":
                    t = ev[1]
                    act.wait_ge(heads_turned, t + 1)
                    if t >= 2:
                        act.wait_ge(projected, t - 1)
                    act.copy(oT_sb[:, t % 2, :], bank[tail_bank(0, t)][:, 0:D]).then_inc(oT_ready, 1)
                if ev[0] == "turn_normal":
                    t = ev[1]
                    act.wait_ge(xhat2_turned, t + 1)
                    if t >= 2:
                        act.wait_ge(gated, t - 1)
                    act.copy(xhat2T[:, t % 2, :], bank[tail_bank(2, t)][:, 0:D]).then_inc(xhat2T_ready, 1)
                if ev[0] == "gate_exp":
                    _, t0, t1 = ev
                    act.wait_ge(top_ready, 1 if t0 == 0 else 2)
                    act.activation(expd[:, t0:t1, :], expd[:, t0:t1, :], ACT.Exp).then_inc(exp_gate, 1)

            def split_weights(e, c):
                if c == 0:
                    act.wait_ge(w_loaded[e % 2], 32 * (e // 2 + 1))
                if e >= 2 and c == 0:
                    act.wait_ge(down_done, CT3 * (e - 1))
                act.copy(chunk(w_split[e % 2][:, 0, :], c), chunk(w_raw[:, e % 2, :], c)).then_inc(w_high, 1)

            def split_slots(e):
                for ft in range(DT):
                    act.wait_ge(slots_turned, e * DT + ft + 1)
                    act.activation(slotT[:, e % 2, 0, ft, :], bank[SLOT_BANKS[ft]][:, 0:CAP], ACT.Identity,
                                   bias=mod_col[:, 2, ft:ft + 1], scale=mod_col[:, 3, ft:ft + 1]).then_inc(slotT_high, 1)

            act.activation(c_tmp[0:1, 2, 0:1], c_tmp[0:1, 0, 0:1], ACT.Gelu)
            act.wait_ge(max_scored, units_before[-1])
            for c in range(CH):
                split_weights(0, c)
            split_slots(0)
            for n in range(E * IT):
                e, it = divmod(n, IT)
                act.wait_ge(up_done, n + 1)
                if n >= AR:
                    m = n - AR
                    act.wait_ge(act_used, (IT - 1) * (m // IT) + min(m % IT + 1, IT - 1))
                    if m % IT == IT - 1:
                        act.wait_ge(down_done, CT3 * (m // IT + 1))
                act.activation(acts[:, n % AR, 0, 0:CAP], bank[n % 3][:, 0:CAP], ACT.Gelu)
                if n >= 2:
                    act.wait_ge(act_ready, n - 1)
                act.activation(act_raw[:, n % 2, :], bank[n % 3][:, 0:CAP], ACT.Gelu).then_inc(gelu_done, 1)
                if e + 1 < E and 2 <= it < 2 + CH:
                    split_weights(e + 1, it - 2)
                if e + 1 < E and it == 0:
                    split_slots(e + 1)

        @block.vector
        def _(dve):
            chain = [0]

            def link(ins):
                chain[0] += 1
                ins.then_inc(dve_chain, 1)
                dve.wait_ge(dve_chain, chain[0])

            dve.wait_ge(c_exp, 1)
            link(dve.tensor_scalar(c_tmp[:, 1, :], c_tmp[:, 0, :], 1.0, None, ALU.add))
            link(dve.reciprocal(c_tmp[:, 2, :], c_tmp[:, 1, :]))
            dve.tensor_tensor(silu[:, :], c_sb[:, :], c_tmp[:, 2, :], ALU.mult).then_inc(silu_ready, 1)

            def inverse_root(ts):
                half, y, y_next = root[:, 0, ts], rstd[:, ts], root[:, 1, ts]
                link(dve.tensor_scalar(y_next, mean_var[:, ts, 1], EPS, None, ALU.add))
                link(dve.tensor_scalar(y_next.bitcast(I32), y_next.bitcast(I32), 1, None, ALU.logical_shift_right))
                link(dve.tensor_scalar(y.bitcast(I32), y_next.bitcast(I32), -1.0, RSQRT_SEED, ALU.mult, ALU.add))
                dve.tensor_scalar(half, mean_var[:, ts, 1], EPS, -0.5, ALU.add, ALU.mult)
                for _ in range(3):
                    link(dve.tensor_tensor(y_next, y, y, ALU.mult))
                    link(dve.tensor_tensor(y_next, y_next, half, ALU.mult))
                    link(dve.scalar_tensor_tensor(out=y, in0=y_next, scalar=1.5, in1=y, op0=ALU.add, op1=ALU.mult))

            def normal(b):
                tiles = range(b * TB, (b + 1) * TB)
                if b <= 2:
                    some = tiles if b < 2 else range(2 * TB, NT)
                    for t in some:
                        if t % TB == 0:
                            dve.wait_ge(loaded_x[t // TB], 16)
                        last = dve.bn_stats(stats[:, t, :], x_sb[:, t, :])
                    link(last)
                    for t in some:
                        last = dve.bn_aggr(mean_var[:, t, :], stats[:, t, :])
                    link(last)
                    inverse_root(slice(some[0], some[-1] + 1))
                if b >= 2:
                    dve.wait_ge(xhat_turned, (b - 1) * DT)
                for t in tiles:
                    dve.tensor_scalar(xhat[:, t % (2 * TB), :], x_sb[:, t, :], mean_var[:, t, 0:1], rstd[:, t:t + 1],
                                      ALU.subtract, ALU.mult).then_inc(xhat_ready, 1)

            def read_mods(first):
                dve.wait_ge(mods_done, 1 if first else 2)
                mods = bank[2 if first else V_BANKS[1]][:, 0:4 * DT].rearrange("p (m t) -> p m t", m=4)
                for m in ((0, 1) if first else (2, 3)):
                    last = dve.tensor_scalar(mod_col[:, m, :], mods[:, m, :], float(m % 2), None, ALU.add)
                last.then_inc(mods_read, 1)
                if first:
                    dve.tensor_copy(bias_all[:, :, :].rearrange("p a d -> p (a d)"), bank[1][:, :]).then_inc(mods_read, 1)
                else:
                    g2 = gates[:, :, :].rearrange("p a d -> p (a d)")
                    s2 = sign[:, :, :].rearrange("p a d -> p (a d)")
                    link(dve.tensor_scalar(s2, bank[V_BANKS[0]][:, :], 0.0, 2.0, ALU.is_ge, ALU.mult))
                    link(dve.tensor_scalar(s2, s2, -1.0, None, ALU.add))
                    link(dve.tensor_tensor(g2, bank[V_BANKS[0]][:, :], s2, ALU.mult))
                    link(dve.tensor_scalar(g2, g2, 0.25, None, ALU.max))
                    dve.tensor_tensor(g2, g2, s2, ALU.mult).then_inc(mods_read, 1)

            def values(b):
                if b == 0:
                    dve.wait_ge(v_zeroed, 1)
                    dve.wait_ge(mods_read, 2)
                for t in range(b * TB, (b + 1) * TB):
                    dve.wait_ge(v_done, t + 1)
                    dve.tensor_tensor(v_sb[:, t, :, 0:HD],
                                      bank[V_BANKS[t % 2]][:, 0:D].rearrange("p (h i) -> p h i", h=H),
                                      bias_all[:, 0, :].rearrange("p (h i) -> p h i", h=H), ALU.add).then_inc(v_read, 1)

            def after_projection(t):
                if t == 0:
                    dve.wait_ge(x_biased, NT)
                dve.wait_ge(projected, t + 1)
                dve.tensor_tensor(x_sb[:, t, :], bank[tail_bank(1, t)][:, 0:D], x_sb[:, t, :], ALU.add)\
                   .then_inc(x1_ready, 1)
                dve.wait_ge(x1_ready, t + 1)
                link(dve.bn_stats(stats[:, t, :], x_sb[:, t, :]))
                link(dve.bn_aggr(mean_var[:, t, :], stats[:, t, :]))
                if t % TB == TB - 1:
                    inverse_root(slice(t + 1 - TB, t + 1))
                    for i in range(t + 1 - TB, t + 1):
                        dve.tensor_scalar(heads[:, i, :], x_sb[:, i, :], mean_var[:, i, 0:1], rstd[:, i:i + 1],
                                          ALU.subtract, ALU.mult).then_inc(xhat2_ready, 1)

            def choose(part_no, t0, t1):
                ts = slice(t0, t1)
                n = t1 - t0

                def wide(a):
                    return a.rearrange("p (t e) -> p t e", e=1).broadcast_to([P, n, E])

                def counts(i):
                    return bank[COUNT_BANK][:, i * NT * E:i * NT * E + n * E].rearrange("p (t e) -> p t e", e=E)
                dve.wait_ge(gated, t1)
                bias = gate_bias[:, :].rearrange("p (t e) -> p t e", t=1).broadcast_to([P, n, E])
                dve.tensor_tensor(logits[:, ts, :], bank[MISC_BANK][:, t0 * E:t1 * E].rearrange("p (t e) -> p t e", e=E),
                                  bias, ALU.add).then_inc(logits_read, 1)
                dve.wait_ge(logits_read, part_no + 1)
                link(dve.tensor_reduce(top[:, ts], logits[:, ts, :], AX.X, ALU.max))
                dve.tensor_tensor(expd[:, ts, :], logits[:, ts, :], wide(top[:, ts]), ALU.subtract).then_inc(top_ready, 1)
                link(dve.tensor_tensor(onehot[:, ts, :], logits[:, ts, :], wide(top[:, ts]), ALU.is_ge))
                link(dve.tensor_tensor(onehot[:, ts, :], onehot[:, ts, :], order[:, ts, :], ALU.mult))
                link(dve.tensor_reduce(top[:, ts], onehot[:, ts, :], AX.X, ALU.max))
                link(dve.tensor_tensor(onehot[:, ts, :], onehot[:, ts, :], wide(top[:, ts]), ALU.is_equal))
                dve.tensor_copy(onehot_b[:, ts, :], onehot[:, ts, :]).then_inc(onehot_ready, 1)
                link(dve.tensor_tensor(logits[:, ts, :], onehot[:, ts, :], limit[:, ts, :], ALU.mult))
                link(dve.tensor_reduce(slot_limit[:, ts], logits[:, ts, :], AX.X, ALU.add))
                dve.wait_ge(exp_gate, part_no + 1)
                link(dve.tensor_reduce(top[:, ts], expd[:, ts, :], AX.X, ALU.add))
                dve.reciprocal(prob[:, ts], top[:, ts])
                dve.wait_ge(counted, part_no + 1)
                for i, t in enumerate(range(t0, t1)):
                    link(dve.tensor_tensor(earlier[:, t + 1, :], earlier[:, t, :], counts(1)[:, i, :], ALU.add))
                dve.tensor_tensor(before[:, ts, :], counts(0), earlier[:, ts, :], ALU.add).then_inc(counts_read, 1)
                dve.wait_ge(counts_read, part_no + 1)
                link(dve.tensor_tensor(before[:, ts, :], before[:, ts, :], onehot[:, ts, :], ALU.mult))
                link(dve.tensor_reduce(slot[:, ts], before[:, ts, :], AX.X, ALU.add))
                link(dve.tensor_tensor(over[:, ts], slot[:, ts], slot_limit[:, ts], ALU.is_ge))
                dve.scalar_tensor_tensor(out=slot_to[:, ts], in0=over[:, ts], scalar=float(NS), in1=slot[:, ts],
                                         op0=ALU.mult, op1=ALU.add).then_inc(slots_known, 1)

            for ev in plan:
                if ev[0] == "normal":
                    normal(ev[1])
                    if ev[1] == 0:
                        dve.wait_ge(pool_consts, 1)
                        dve.wait_ge(silu_ready, 1)
                        for ft in range(DT):
                            last = dve.tensor_scalar(silu_rep[:, ft, :], ones_f[:, :], silu[:, ft:ft + 1], None, ALU.mult)
                        dve.wait_ge(loaded_qkv, 48)
                        link(last)
                        dve.tensor_scalar(b_qk_sb[:, :], b_qk_sb[:, :], qk_scale[:, 0:1], None, ALU.mult)\
                           .then_inc(silu_ready, 1)
                        read_mods(True)
                if ev[0] == "first_qk":
                    leave_part0(dve, ev[1], rest_ready_v)
                    leave_part1(dve, ev[1], qk_split_v)
                if ev[0] == "values":
                    values(ev[1])
                if ev[0] == "mods":
                    read_mods(False)
                if ev[0] == "gate_bias":
                    dve.wait_ge(mods_read, 4)
                    for ft in range(DT):
                        shift = dve.tensor_scalar(product[:, 0, ft * P:(ft + 1) * P], ones_f[:, :],
                                                  mod_col[:, 2, ft:ft + 1], None, ALU.mult)
                    shift.then_inc(gate_rows_ready, 1)
                    dve.wait_ge(misc_done, misc_use[ev] + 1)
                    dve.tensor_copy(gate_bias[:, :], bank[MISC_BANK][:, 0:E]).then_inc(misc_read_v, 1)
                    for ft in range(DT):
                        scaled = dve.tensor_scalar(w_gate_sb[:, ft, :], w_gate_sb[:, ft, :], mod_col[:, 3, ft:ft + 1],
                                                   None, ALU.mult)
                    scaled.then_inc(w_gate_ready, 1)
                if ev[0] == "max":
                    _, u, g, b, qt, h, c, width = ev
                    n = g * NB + b
                    src = bank[MAX_BANKS[u % 3]]
                    to = chunk_max[:, n % 2, qt * HG + h, c:c + 1]
                    dve.wait_ge(max_scored, u + 1)
                    if c < b:
                        dve.tensor_reduce(to, src[:, 0:QB], AX.X, ALU.max).then_inc(max_read, 1)
                    else:
                        if u >= 3:
                            dve.wait_ge(max_read, u - 2)
                        if u == 0:
                            dve.wait_ge(causal_ready, 1)
                        dve.tensor_tensor_reduce(out=masked[:, u % 3, 0:width], in0=src[:, 0:width],
                                                 in1=causal[:, QB - width:QB], scale=1.0, scalar=NEG, op0=ALU.add,
                                                 op1=ALU.max, accum_out=to).then_inc(max_read, 1)
                if ev[0] == "max_parts":
                    n = ev[1]
                    b = n % NB
                    dve.wait_ge(max_read, units_before[n + 1])
                    link(dve.tensor_reduce(neg_max[:, :], chunk_max[:, n % 2, :, 0:b + 1], AX.X, ALU.max, negate=True))
                    if n >= 2:
                        dve.wait_ge(misc_done, misc_use["max_rows", n - 2] + 1)
                    link(dve.tensor_copy(max_part[:, n % 2, :, 0], neg_max[:, :]))
                    dve.tensor_tensor(max_part[:, n % 2, :, 1], neg_max[:, :], max_part[:, n % 2, :, 0], ALU.subtract)\
                        .then_inc(max_parts, 1)
                if ev[0] == "max_rows":
                    n = ev[1]
                    g, b = divmod(n, NB)
                    rows = stack(g, 0)[KR:KR + MR, :, b * QB:(b + 1) * QB]
                    dve.wait_ge(max_row0, n + 1)
                    dve.tensor_copy(rows[:, 1:HG, :], rows[:, 0:1, :].broadcast_to([MR, HG - 1, QB]))\
                        .then_inc(max_rows, 1)
                if ev[0] == "turn_heads":
                    n = ev[1]
                    g, b = divmod(n, NB)
                    dve.wait_ge(misc_done, misc_use[ev] + 1)
                    o = bank[MISC_BANK][:, :].rearrange("p (t h c) -> p t h c", t=TB, h=HG)
                    inv = inv_sum[:, :].rearrange("p (t h) -> p t h", t=TB)
                    link(dve.reciprocal(inv, o[:, :, :, HD]))
                    to = heads[:, b * TB:(b + 1) * TB, g * HG * HD:(g + 1) * HG * HD]
                    dve.tensor_tensor(to.rearrange("p t (h i) -> p t h i", h=HG), o[:, :, :, 0:HD],
                                      inv.rearrange("p t (h i) -> p t h i", i=1).broadcast_to([P, TB, HG, HD]), ALU.mult)\
                        .then_inc(misc_read_v, 1)
                if ev[0] == "out":
                    after_projection(ev[1])
                if ev[0] == "rank":
                    choose(0 if ev[1] == 0 else 1, ev[1], ev[2])

            def split_weights(e, c):
                dve.wait_ge(w_high, CH * e + c + 1)
                dve.tensor_tensor(chunk(w_split[e % 2][:, 1, :], c), chunk(w_raw[:, e % 2, :], c),
                                  chunk(w_split[e % 2][:, 0, :], c).bitcast(F32), ALU.subtract).then_inc(w_ready, 1)

            def split_slots(e, ft):
                k = e * DT + ft
                dve.wait_ge(slotT_high, k + 1)
                dve.tensor_scalar(slotT_raw[:, ft, :], bank[SLOT_BANKS[ft]][:, 0:CAP], mod_col[:, 3, ft:ft + 1],
                                  mod_col[:, 2, ft:ft + 1], ALU.mult, ALU.add).then_inc(slotT_raw_done, 1)
                dve.wait_ge(slotT_raw_done, k + 1)
                dve.tensor_tensor(slotT[:, e % 2, 1, ft, :], slotT_raw[:, ft, :],
                                  slotT[:, e % 2, 0, ft, :].bitcast(F32), ALU.subtract).then_inc(slotT_ready, 1)

            def finish_rows(e):
                if e >= 2:
                    dve.wait_ge(rows_stored[e % 2], 16 * CT3 * (e // 2))
                for st in range(CT3):
                    k = CT3 * e + st
                    r = slice(0, rows_of(st))
                    dve.wait_ge(down_done, k + 1)
                    dve.scalar_tensor_tensor(out=down[r, e % 2, st, :], in0=bank[DOWN_BANKS[st]][r, 0:D],
                                             scalar=slots_sb[r, e % SR, st, 2 * D:2 * D + 1], in1=gates[r, 1, :],
                                             op0=ALU.mult, op1=ALU.mult).then_inc(down_read, 1)

            def add_rows(e, st):
                r = slice(0, rows_of(st))
                dve.wait_ge(down_read, CT3 * e + st + 1)
                dve.tensor_tensor(down[r, e % 2, st, :], down[r, e % 2, st, :], slots_sb[r, e % SR, st, 0:D],
                                  ALU.add).then_inc(rows_ready, 1)

            ADD_AT = (DOWN_LAG - 1, IT - 2, IT - 1)
            dve.memset(acts[:, :, :, CAP:CAPW].bitcast(F32), 0.0).then_inc(pads_zeroed, 1)
            for c in range(CH):
                split_weights(0, c)
            for ft in range(DT):
                split_slots(0, ft)
            for n in range(E * IT):
                e, it = divmod(n, IT)
                dve.wait_ge(gelu_done, n + 1)
                dve.tensor_tensor(acts[:, n % AR, 1, 0:CAP], act_raw[:, n % 2, :], acts[:, n % AR, 0, 0:CAP].bitcast(F32),
                                  ALU.subtract).then_inc(act_ready, 1)
                if it == DOWN_LAG - 1 and e >= 1:
                    finish_rows(e - 1)
                if it in ADD_AT and e >= 1:
                    add_rows(e - 1, ADD_AT.index(it))
                if e + 1 < E:
                    if 2 <= it < 2 + CH:
                        split_weights(e + 1, it - 2)
                    if it in (0, IT - 2):
                        split_slots(e + 1, 0 if it == 0 else 1)
            finish_rows(E - 1)
            for st in range(CT3):
                add_rows(E - 1, st)

        @block.tensor
        def _(pe):
            pe.wait_ge(pool_consts, 1)
            pe.wait_ge(silu_ready, 1)
            pe.wait_ge(loaded_shift, 32)

            def column_mods(out, pairs):
                for j, m in pairs:
                    for ft in range(DT):
                        for k in range(DT):
                            mm = pe.matmul(out[:, j * DT + ft:j * DT + ft + 1],
                                           w_mod_sb[:, k, m * D + ft * P:m * D + (ft + 1) * P], silu[:, k:k + 1],
                                           start=(k == 0), stop=(k == DT - 1))
                return mm
            pe.matmul(bank[1][:, :], ones_f[0:1, :], bias_row.rearrange("a t d -> a (t d)"), start=True, stop=True)
            column_mods(bank[2], ((0, 0), (1, 1))).then_inc(mods_done, 1)

            def misc_free(ev):
                a, v = misc_reads(misc_use[ev])
                if a:
                    pe.wait_ge(misc_read_a, a)
                if v:
                    pe.wait_ge(misc_read_v, v)

            def project(g, b, piece):
                if piece == 0:
                    misc_free(("project", g, b))
                width = QB // PIECES
                at = piece * width
                for k in range(DT):
                    mm = pe.matmul(bank[MISC_BANK][:, at:at + width], w_qk_sb[:, k, g * P:(g + 1) * P],
                                   hT[:, k, b * QB + at:b * QB + at + width], start=(k == 0), stop=(k == DT - 1))
                if piece == PIECES - 1:
                    mm.then_inc(misc_done, 1)

            def turn_x(b):
                pe.wait_ge(xhat_ready, (b + 1) * TB)
                if b >= 1:
                    pe.wait_ge(hT_ready, b * DT)
                for ft in range(DT):
                    for t in range(TB):
                        mm = pe.transpose(bank[TURN_BANKS[ft]][:, t * P:(t + 1) * P],
                                          xhat[:, (b * TB + t) % (2 * TB), ft * P:(ft + 1) * P], ident[:, :])
                    mm.then_inc(xhat_turned, 1)

            def first_qk(b):
                if b == 0:
                    pe.wait_ge(loaded_qkv, 48)
                pe.wait_ge(hT_ready, (b + 1) * DT)
                for piece in range(PIECES):
                    project(0, b, piece)

            def values(b):
                pe.wait_ge(hT_ready, (b + 1) * DT)
                for t in range(b * TB, (b + 1) * TB):
                    if t >= 2:
                        pe.wait_ge(v_read, t - 1)
                    for k in range(DT):
                        mm = pe.matmul(bank[V_BANKS[t % 2]][:, 0:D], hT[:, k, t * P:(t + 1) * P], w_v_sb[:, k, :],
                                       start=(k == 0), stop=(k == DT - 1))
                    mm.then_inc(v_done, 1)

            def turn_heads(n):
                pe.wait_ge(o_read, n + 1)
                misc_free(("turn_heads", n))
                if n == NG * NB - 1:
                    pe.wait_ge(logits_read, 1)
                for t in range(TB):
                    mm = pe.transpose(bank[MISC_BANK][:, t * P:(t + 1) * P], o_sb[:, n % 2, t * P:(t + 1) * P], ident[:, :])
                mm.then_inc(misc_done, 1)

            def weigh_values(n, kt):
                s = step_of[n, kt]
                j = kt - (n % NB) * TB
                if j >= 0:
                    pe.wait_ge(diag_done, n * TB + j + 1)
                else:
                    pe.wait_ge(exp_done, HG * (s + 1))
                first, last = kt == key_tiles(n % NB)[0], kt == key_tiles(n % NB)[-1]
                if first and n >= 1:
                    pe.wait_ge(o_read, n)
                lo = P * max(0, j)
                g = n // NB
                for h in range(HG):
                    mm = pe.matmul(bank[VALUE_BANK][CT * h:CT * (h + 1), lo:QB], v_sb[:, kt, g * HG + h, :],
                                   probs[:, s % 3, h, 0:QB - lo], start=first, stop=last,
                                   skip_group_check=True)
                mm.then_inc(weighted, 1)

            def emptied(ready, t):
                last = t if t <= TAIL_TILES else t - 1
                if last:
                    pe.wait_ge(ready, last)

            for ev in plan:
                if ev[0] == "turn_x":
                    turn_x(ev[1])
                if ev[0] == "first_qk":
                    first_qk(ev[1])
                if ev[0] == "values":
                    values(ev[1])
                if ev[0] == "mods":
                    pe.wait_ge(loaded_mod, 16)
                    pe.wait_ge(silu_ready, 2)
                    pe.wait_ge(v_read, NT)
                    column_mods(bank[V_BANKS[1]], ((2, 3), (3, 4)))
                    for j, m in enumerate((2, 5)):
                        for k in range(DT):
                            mm = pe.matmul(bank[V_BANKS[0]][:, j * D:(j + 1) * D], silu_rep[:, k, :],
                                           w_mod_sb[:, k, m * D:(m + 1) * D], start=(k == 0), stop=(k == DT - 1))
                    mm.then_inc(mods_done, 1)
                if ev[0] == "gate_bias":
                    pe.wait_ge(gate_rows_ready, 1)
                    pe.wait_ge(loaded_late, 32)
                    misc_free(ev)
                    for k in range(DT):
                        mm = pe.matmul(bank[MISC_BANK][:, 0:E], product[:, 0, k * P:(k + 1) * P], w_gate_sb[:, k, :],
                                       start=(k == 0), stop=(k == DT - 1))
                    mm.then_inc(misc_done, 1)
                if ev[0] == "max":
                    _, u, g, b, qt, h, c, width = ev
                    if u == 0:
                        pe.wait_ge(mods_read, 2)
                    if (qt, h, c) == (0, 0, 0):
                        if g == 0:
                            pe.wait_ge(stacked_first[b], 16 * STACK_DMAS)
                        elif b == 0:
                            pe.wait_ge(stacked[g], 16 * STACK_DMAS)
                    if u >= 3:
                        pe.wait_ge(max_read, u - 2)
                    q0 = b * QB + qt * P
                    pe.matmul(bank[MAX_BANKS[u % 3]][:, 0:width], stack(g, 0)[0:KR, h, q0:q0 + P],
                              stack(g, 1)[0:KR, h, c * QB:c * QB + width], start=True, stop=True).then_inc(max_scored, 1)
                if ev[0] == "max_rows":
                    n = ev[1]
                    pe.wait_ge(max_parts, n + 1)
                    misc_free(ev)
                    for t in range(TB):
                        mm = pe.transpose(bank[MISC_BANK][:, :].bitcast(BF16)[0:MR, t * P:(t + 1) * P],
                                          max_part[:, n % 2, t * HG:(t + 1) * HG, :].rearrange("p h a -> p (h a)"),
                                          ident_b[:, :])
                    mm.then_inc(misc_done, 1)
                if ev[0] == "project":
                    project(*ev[1:])
                if ev[0] == "scores":
                    _, n, kt, h = ev
                    g, b = divmod(n, NB)
                    u = HG * step_of[n, kt] + h
                    lo = P * max(0, kt - b * TB)
                    if kt == key_tiles(b)[0] and h == 0:
                        pe.wait_ge(max_rows, n + 1)
                        if n == 0:
                            pe.wait_ge(hT_ready, NB * DT)
                            pe.wait_ge(mods_read, 4)
                        if b == 0 and g == 0:
                            pe.wait_ge(ones_rows, HG)
                        if b == 0 and g == 1:
                            pe.wait_ge(ones_copied, 16)
                    if u >= 3:
                        pe.wait_ge(exp_done, u - 2)
                    pe.matmul(bank[SCORE_BANKS[u % 3]][:, 0:QB - lo], stack(g, 1)[0:KR + MR, h, kt * P:(kt + 1) * P],
                              stack(g, 0)[0:KR + MR, h, b * QB + lo:(b + 1) * QB], start=True, stop=True)\
                        .then_inc(scored, 1)
                if ev[0] == "weigh":
                    weigh_values(ev[1], ev[2])
                if ev[0] == "turn_heads":
                    turn_heads(ev[1])
                if ev[0] == "turn":
                    t = ev[1]
                    if t == 0:
                        pe.wait_ge(max_read, units_before[-1])
                    emptied(oT_ready, t)
                    pe.wait_ge(misc_read_v, heads_read((NG - 1) * NB + t // TB))
                    for ft in range(DT):
                        mm = pe.transpose(bank[tail_bank(0, t)][:, ft * P:(ft + 1) * P], heads[:, t, ft * P:(ft + 1) * P],
                                          ident[:, :])
                    mm.then_inc(heads_turned, 1)
                if ev[0] == "out":
                    t = ev[1]
                    if t == 0:
                        pe.wait_ge(w_o_ready, 1)
                    emptied(x1_ready, t)
                    pe.wait_ge(oT_ready, t + 1)
                    for k in range(DT):
                        mm = pe.matmul(bank[tail_bank(1, t)][:, 0:D], oT_sb[:, t % 2, k * P:(k + 1) * P], w_o_sb[:, k, :],
                                       start=(k == 0), stop=(k == DT - 1))
                    mm.then_inc(projected, 1)
                if ev[0] == "turn_normal":
                    t = ev[1]
                    if t == TAIL_TILES:
                        pe.wait_ge(counts_read, 1)
                    emptied(xhat2T_ready, t)
                    pe.wait_ge(xhat2_ready, t + 1)
                    for ft in range(DT):
                        mm = pe.transpose(bank[tail_bank(2, t)][:, ft * P:(ft + 1) * P], heads[:, t, ft * P:(ft + 1) * P],
                                          ident[:, :])
                    mm.then_inc(xhat2_turned, 1)
                if ev[0] == "gate":
                    t = ev[1]
                    if t == 0 or t == TAIL_TILES:
                        pe.wait_ge(misc_read_v, heads_read(NG * NB - (2 if t == 0 else 1)))
                    if t == 0:
                        pe.wait_ge(w_gate_ready, 1)
                    pe.wait_ge(xhat2T_ready, t + 1)
                    for k in range(DT):
                        mm = pe.matmul(bank[MISC_BANK][:, t * E:(t + 1) * E], xhat2T[:, t % 2, k * P:(k + 1) * P],
                                       w_gate_sb[:, k, :], start=(k == 0), stop=(k == DT - 1))
                    mm.then_inc(gated, 1)
                if ev[0] == "rank":
                    _, t0, t1 = ev
                    pe.wait_ge(onehot_ready, 1 if t0 == 0 else 2)
                    pe.wait_ge(xhat2T_ready, t1)
                    chosen = onehot_b[:, t0:t1, :].rearrange("p t e -> p (t e)")
                    for i, w in enumerate((upper, ones_b)):
                        mm = pe.matmul(bank[COUNT_BANK][:, i * NT * E:i * NT * E + (t1 - t0) * E], w[:, :], chosen,
                                       start=True, stop=True)
                    mm.then_inc(counted, 1)

            def turn_slots(e):
                pe.wait_ge(slots_loaded[e % SR], 32 * (e // SR + 1))
                if e >= 1:
                    pe.wait_ge(slotT_high, DT * e)
                    pe.wait_ge(slotT_raw_done, DT * e)
                for ft in range(DT):
                    for st in range(CT3):
                        rows = rows_of(st)
                        mm = pe.transpose(bank[SLOT_BANKS[ft]][:, st * P:st * P + rows],
                                          slots_sb[0:rows, e % SR, st, D + ft * P:D + (ft + 1) * P], ident[0:rows, 0:rows])
                    mm.then_inc(slots_turned, 1)

            PAIRS = ((1, 0), (0, 1), (0, 0))

            def up(n):
                e, it = divmod(n, IT)
                if it == 0:
                    pe.wait_ge(w_ready, CH * e + CH // 2)
                    pe.wait_ge(slotT_ready, DT * (e + 1))
                if n >= 3:
                    pe.wait_ge(gelu_done, n - 2)
                for i, (a, b) in enumerate(PAIRS):
                    for k in range(DT):
                        col = k * I + it * P
                        mm = pe.matmul(bank[n % 3][:, 0:CAP], w_split[e % 2][:, a, col:col + P],
                                       slotT[:, e % 2, b, k, :], start=(i == 0 and k == 0),
                                       stop=(i == len(PAIRS) - 1 and k == DT - 1))
                mm.then_inc(up_done, 1)

            def down_to(n):
                e, it = divmod(n, IT)
                if it == 0:
                    pe.wait_ge(w_ready, CH * (e + 1))
                if n == 0:
                    pe.wait_ge(pads_zeroed, 1)
                pe.wait_ge(act_ready, n + 1)
                col = DT * I + it * D
                for st in range(CT3):
                    if it == 0 and e >= 1:
                        pe.wait_ge(down_read, CT3 * (e - 1) + st + 1)
                    for i, (a, b) in enumerate(PAIRS):
                        mm = pe.matmul(bank[DOWN_BANKS[st]][:, 0:D], acts[:, n % AR, a, st * P:(st + 1) * P],
                                       w_split[e % 2][:, b, col:col + D], start=(it == 0 and i == 0),
                                       stop=(it == IT - 1 and i == len(PAIRS) - 1))
                    if it == IT - 1:
                        mm.then_inc(down_done, 1)
                if it < IT - 1:
                    mm.then_inc(act_used, 1)

            pe.wait_ge(slots_known, 2)
            turn_slots(0)
            for n in range(E * IT):
                up(n)
                if n % IT == 0 and n // IT + 1 < E:
                    turn_slots(n // IT + 1)
                if n >= DOWN_LAG:
                    down_to(n - DOWN_LAG)
            for n in range(E * IT - DOWN_LAG, E * IT):
                down_to(n)


def kernel(L0_attn_x, L0_attn_w_qkv, L0_attn_b_qkv, L0_attn_w_out, L0_attn_b_out, L0_ffn_gate_weight, L0_ffn_wi,
           L0_ffn_wo, L0_c, L0_wmod):
    import numpy as np
    import concourse.bacc as bacc
    from concourse.bass_utils import run_bass_kernel_spmd

    w_qkv, b_qkv = np.asarray(L0_attn_w_qkv), np.asarray(L0_attn_b_qkv)
    q, k = (w_qkv[i * D:(i + 1) * D].reshape(NG, HG, HD, D).swapaxes(1, 2).reshape(NG, HG * HD, D) for i in range(2))
    bq, bk = (b_qkv[i * D:(i + 1) * D].reshape(NG, HG, HD).swapaxes(1, 2).reshape(NG, HG * HD) for i in range(2))
    arrays = {
        "x": np.asarray(L0_attn_x)[0],
        "w_qk": np.concatenate([q, k], axis=1).reshape(NG * P, D).T,
        "b_qk": np.concatenate([bq, bk], axis=1).T,
        "w_v": w_qkv[2 * D:].T,
        "w_o": np.asarray(L0_attn_w_out).T,
        "b_rows": np.stack([b_qkv[2 * D:], np.asarray(L0_attn_b_out)]),
        "w_gate": np.asarray(L0_ffn_gate_weight).T,
        "w_in": np.asarray(L0_ffn_wi),
        "w_down": np.asarray(L0_ffn_wo),
        "c_col": np.asarray(L0_c)[0].reshape(DT, P).T,
        "w_mod": np.asarray(L0_wmod),
    }
    arrays = {n: np.ascontiguousarray(a) for n, a in arrays.items()}
    nc = bacc.Bacc("TRN2", target_bir_lowering=False, num_devices=1)
    args = {n: nc.dram_tensor(n, a.shape, mybir.dt.from_np(a.dtype), kind="ExternalInput").ap()
            for n, a in arrays.items()}
    result = nc.dram_tensor("out", (S, D), F32, kind="ExternalOutput").ap()
    layer(nc, *args.values(), result)
    r = run_bass_kernel_spmd(nc, [arrays], core_ids=[0])
    return r.results[0]["out"].reshape(1, S, D)
```
